# Optimizing a Trainium2 kernel written in Bass

```python
import numpy as np
import jax
import jax.numpy as jnp

def _softmax(x, axis=-1):
    return jax.nn.softmax(x, axis=axis)

def _gelu(x):
    return jax.nn.gelu(x, approximate=True)

def _silu(x):
    return jax.nn.silu(x)

def _sigmoid(x):
    return jax.nn.sigmoid(x)

def _layernorm(x, axis=-1, eps=1e-05):
    m = jnp.mean(x, axis=axis, keepdims=True)
    v = jnp.var(x, axis=axis, keepdims=True)
    return (x - m) / jnp.sqrt(v + eps)

def _scatter_add(tgt, idx, src, axis=0):
    return tgt.at[idx].add(src)

def _segment_sum(src, seg, n):
    return jax.ops.segment_sum(src, seg, n)
kernel_name = 'mk_adaln_ffn_d1_seqx_r4_1ecc4f'

def setup_inputs(seed: int=0):
    np.random.seed(seed)
    _w = jnp.asarray

    def _rec_inputs():
        import jax
        import jax.numpy as jnp
        _rk = jax.random.key(seed)
        x = 7.22e-05 + 1 * jax.random.normal(jax.random.fold_in(_rk, 1), (8, 256, 1024), jnp.float32)
        _lenS = 256 - jax.random.randint(jax.random.fold_in(_rk, 7), (8,), 0, max(1, 256 // 4) + 1, jnp.int32)
        _lenS2 = 256 - jax.random.randint(jax.random.fold_in(_rk, 8), (8,), 0, max(1, 256 // 4) + 1, jnp.int32)
        itok_B_2_6 = jax.random.randint(jax.random.fold_in(_rk, 11), (8,), 2, 7, jnp.int32)
        return (x, itok_B_2_6)
    x, itok_B_2_6 = _rec_inputs()

    def _L0_cond_setup():
        import jax, jax.numpy as jnp
        import numpy as np
        B, N, H, F = (4, 128, 1024, 2752)
        L, R, RANK = (1, 16, 16)
        SCALE = 0.5
        key = jax.random.key(seed)
        ks = jax.random.split(key, 12)
        nrm = lambda k, shape, fan: jax.random.normal(k, shape, jnp.float32) * fan ** (-0.5)
        inp = {'x': jax.random.normal(ks[0], (B, N, H), jnp.float32), 'W_gate': nrm(ks[1], (F, H), H), 'W_up': nrm(ks[2], (F, H), H), 'W_down': nrm(ks[3], (H, F), F), 'A_gate': nrm(ks[4], (L, R, RANK, H), H), 'B_gate': nrm(ks[5], (L, R, F, RANK), RANK), 'A_up': nrm(ks[6], (L, R, RANK, H), H), 'B_up': nrm(ks[7], (L, R, F, RANK), RANK), 'A_down': nrm(ks[8], (L, R, RANK, F), F), 'B_down': nrm(ks[9], (L, R, H, RANK), RANK), 'lora_indices': jax.random.randint(ks[10], (B,), 0, R), 'layer_idx': 0}
        return inp
    _L0_cond_all = _L0_cond_setup()
    _L0_cond_in = {k: v for k, v in _L0_cond_all.items() if k in ('W_gate', 'W_up', 'W_down', 'A_gate', 'B_gate', 'A_up', 'B_up', 'A_down', 'B_down')}
    del _L0_cond_all

    def _L0_ffn_setup():
        import jax, jax.numpy as jnp
        import numpy as np
        TOP_K = 2
        key = jax.random.key(seed)
        k0, k1, k2 = jax.random.split(key, 3)
        B, S, D, H, E = (4, 512, 1024, 1024, 8)
        sc = 1.0 / np.sqrt(D).astype(np.float32)
        x = jax.random.normal(k0, (B, S, D), dtype=jnp.float32)
        W_gate = jax.random.normal(k1, (D, E), dtype=jnp.float32) * sc
        b_gate = jnp.zeros((E,), dtype=jnp.float32)
        W_e = jax.random.normal(k2, (E, D, H), dtype=jnp.float32) * sc
        b_e = jnp.zeros((E, H), dtype=jnp.float32)
        return {'x': x, 'W_gate': W_gate, 'b_gate': b_gate, 'W_e': W_e, 'b_e': b_e}
    _L0_ffn_all = _L0_ffn_setup()
    _L0_ffn_in = {k: v for k, v in _L0_ffn_all.items() if k in ('W_gate', 'b_gate', 'W_e', 'b_e')}
    del _L0_ffn_all
    return {'x': x, 'itok_B_2_6': itok_B_2_6, 'L0_cond_W_gate': _L0_cond_in['W_gate'], 'L0_cond_W_up': _L0_cond_in['W_up'], 'L0_cond_W_down': _L0_cond_in['W_down'], 'L0_cond_A_gate': _L0_cond_in['A_gate'], 'L0_cond_B_gate': _L0_cond_in['B_gate'], 'L0_cond_A_up': _L0_cond_in['A_up'], 'L0_cond_B_up': _L0_cond_in['B_up'], 'L0_cond_A_down': _L0_cond_in['A_down'], 'L0_cond_B_down': _L0_cond_in['B_down'], 'L0_ffn_W_gate': _L0_ffn_in['W_gate'], 'L0_ffn_b_gate': _L0_ffn_in['b_gate'], 'L0_ffn_W_e': _L0_ffn_in['W_e'], 'L0_ffn_b_e': _L0_ffn_in['b_e']}

def reference(x, itok_B_2_6, L0_cond_W_gate, L0_cond_W_up, L0_cond_W_down, L0_cond_A_gate, L0_cond_B_gate, L0_cond_A_up, L0_cond_B_up, L0_cond_A_down, L0_cond_B_down, L0_ffn_W_gate, L0_ffn_b_gate, L0_ffn_W_e, L0_ffn_b_e):
    import jax
    import jax.numpy as jnp

    def _L0_cond_ref(x, W_gate, W_up, W_down, A_gate, B_gate, A_up, B_up, A_down, B_down, lora_indices, layer_idx):
        import jax, jax.numpy as jnp
        import numpy as np
        B, N, H, F = (4, 128, 1024, 2752)
        L, R, RANK = (1, 16, 16)
        SCALE = 0.5

        def lora_add(base, inp, A, B):
            Ab = A[layer_idx][lora_indices]
            Bb = B[layer_idx][lora_indices]
            t = jnp.einsum('bri,bni->bnr', Ab, inp)
            return base + jnp.einsum('bor,bnr->bno', Bb, t) * SCALE
        gate = lora_add(jnp.einsum('bnh,fh->bnf', x, W_gate), x, A_gate, B_gate)
        up = lora_add(jnp.einsum('bnh,fh->bnf', x, W_up), x, A_up, B_up)
        act = jax.nn.silu(gate) * up
        down = lora_add(jnp.einsum('bnf,hf->bnh', act, W_down), act, A_down, B_down)
        return down

    def _L0_ffn_ref(x, W_gate, b_gate, W_e, b_e):
        import jax, jax.numpy as jnp
        import numpy as np
        TOP_K = 2
        logits = x @ W_gate + b_gate
        _, top_idx = jax.lax.top_k(logits, TOP_K)
        y_all = jax.nn.relu(jnp.einsum('bsd,edh->bseh', x, W_e) + b_e)
        y = jnp.take_along_axis(y_all, top_idx[..., None], axis=2)
        return y.mean(axis=2)
    x = x + _L0_ffn_ref(_L0_cond_ref(x, L0_cond_W_gate, L0_cond_W_up, L0_cond_W_down, L0_cond_A_gate, L0_cond_B_gate, L0_cond_A_up, L0_cond_B_up, L0_cond_A_down, L0_cond_B_down, itok_B_2_6, 0), L0_ffn_W_gate, L0_ffn_b_gate, L0_ffn_W_e, L0_ffn_b_e)
    return x

_drawn_inputs = setup_inputs


def setup_inputs(seed=0):
    import zlib

    import numpy as np

    out = dict(_drawn_inputs(seed))
    spreads = {'L0_ffn_b_gate': (0.0, 0.1), 'L0_ffn_b_e': (0.0, 0.1)}
    factors = {}
    for name, (base, spread) in spreads.items():
        noise = np.random.default_rng([zlib.crc32(name.encode()), seed]).standard_normal(out[name].shape)
        drawn = base * np.exp(spread * noise) if base else spread * noise
        out[name] = jnp.asarray(drawn.astype(out[name].dtype))
    for name, factor in factors.items():
        out[name] = (out[name] * factor).astype(out[name].dtype)
    return out
```

```python
from contextlib import ExitStack

import concourse.bass as bass
from concourse import mybir

F32 = mybir.dt.float32
F32R = mybir.dt.float32r
BF16 = mybir.dt.bfloat16
I32 = mybir.dt.int32
U32 = mybir.dt.uint32
ALU = mybir.AluOpType
ACT = mybir.ActivationFunctionType
AX = mybir.AxisListType

T = 2048
H = 1024
F = 2752
NG = 4
NC = 22
NU = 65
S2 = 43
NE = 8
NB = 39
NBP = 40
RW = 3
XAT = [S2 + 4, S2 + 7, S2 + 10, S2 + 13]


EARLY = {(0, 0): S2 + 3, (0, 1): S2 + 5, (0, 2): S2 + 7, (0, 3): S2 + 9, (0, 4): S2 + 15, (0, 5): S2 + 16,
         (0, 6): S2 + 17, (0, 7): S2 + 18, (1, 0): S2 + 19, (1, 1): S2 + 20, (1, 2): S2 + 21}


class Jobs:

    def __init__(self):
        self.jobs = []

    def add(self, key, fn, *args):
        self.jobs.append((key, len(self.jobs), fn, args))

    def run(self, eng):
        for _, _, fn, args in sorted(self.jobs, key=lambda j: j[:2]):
            fn(eng, *args)


def unit_gate(g, c):
    return g * NU + 2 * c


def unit_up(g, c):
    return g * NU + (2 * c + 1 if c < NC - 1 else 2 * c)


def unit_down(g, h, j):
    return g * NU + S2 + 11 * h + j


def piece_list():
    out = [("w", 0, 0)] + [("x", 0, i) for i in range(4)]
    for g in range(NG):
        for n in range(NU):
            if g + 1 < NG and n in XAT:
                out.append(("x", g + 1, XAT.index(n)))
            if g == NG - 1:
                out += [("e", e, k) for e, k in EARLY if EARLY[e, k] == n]
            if (g, n) != (0, 0):
                out.append(("w", g, n))
    for e in range(NE):
        for k in range(8):
            if (e, k) not in EARLY:
                out.append(("e", e, k))
    return out


def build(nc, xp, xn, wp, agu, bgu, bdn, itok, wgt, bg, we, be, cst_f, cst_i, ident_d, ut_d, out):
    pieces = piece_list()
    at = {p: i for i, p in enumerate(pieces)}
    LT = [(q, h, h) for q in range(12) for h in range(2)]
    LT += [(12 + t, 0, t % 2) for t in range(4)] + [(12 + t, 1, t % 2) for t in range(4)]
    LT_AT = {(q, h): m for m, (q, h, _) in enumerate(LT)}
    NP = len(pieces)

    ctx = ExitStack()
    with ctx:
        def sb(name, shape, dt):
            return ctx.enter_context(nc.sbuf_tensor(name, shape, dt))

        def sem(name):
            return ctx.enter_context(nc.semaphore(name))

        XO, AO = 0, 8192
        BO = AO + 21 * 1024 + 512
        LO = BO + 2 * 512
        LA = 38 * 32 + 96
        RN = LO + 2 * LA
        R = sb("R", [128, RN], F32R)
        ring = sb("ring", [128, RW * 2048], F32R)
        TT = sb("TT", [96, 3, 512], F32R)
        raw = sb("raw", [128, RW, 1024], F32)
        braw = sb("braw", [96, 2, 512], F32)
        araw = sb("araw", [128, 2, 608], F32)
        ybuf = sb("ybuf", [128, 4, 1024], F32)
        sbuf2 = sb("sbuf2", [128, 4, 512], F32)
        ytp = sb("ytp", [128, 1024], F32)
        ident = sb("ident", [128, 128], F32)
        ut = sb("ut", [128, 256], BF16)
        cf = sb("cf", [128, 512], F32)
        ci = sb("ci", [128, 32], F32)
        wg_s = sb("wg_s", [128, 8, 8], F32)
        bg_s = sb("bg_s", [128, 8], F32)
        Lg = sb("Lg", [128, 16, 8], F32)
        mx = sb("mx", [128, 16, 8], F32)
        mi = sb("mi", [128, 16, 8], U32)
        lorai = sb("lorai", [128, 8], I32)
        loraf = sb("loraf", [128, 8], F32)
        idx_a = sb("idx_a", [128, 8], U32)
        idx_b = sb("idx_b", [128, 8, NC], U32)
        idx_d = sb("idx_d", [128, 8, 2], U32)
        gidx = sb("gidx", [128, NBP], U32)
        sidx = sb("sidx", [128, NBP], U32)
        meta = sb("meta", [128, 128], I32)
        oE = sb("oE", [128, NBP], F32R)
        msk = sb("msk", [128, 16, 8], BF16)
        posi = sb("posi", [128, 3, 32], U32)
        PS = ctx.enter_context(nc.psum_tensor("PS", [128, 8, 512], F32))

        def x_t(part, k):
            return R[:, XO + part * 4096 + k * 512: XO + part * 4096 + (k + 1) * 512]

        def act_t(c, part):
            o = AO + c * 1024 + part * 512
            return R[:, o:o + 512]

        def b_t(slot):
            return R[0:96, BO + slot * 512: BO + (slot + 1) * 512]

        def a_t(b):
            return R[:, LO + b * LA: LO + (b + 1) * LA]

        def ring_t(n, part):
            o = (n % RW) * 2048 + part * 1024
            return ring[:, o:o + 1024]

        def s_w_t(e, k, part):
            o = (e % 2) * 16384 + k * 2048 + part * 1024
            return R[:, o:o + 1024]

        s_c = sem("s_c")
        s_cb = sem("s_cb")
        s_init = sem("s_init")
        s_idx = sem("s_idx")
        s_raw = [sem(f"s_raw{i}") for i in range(RW)]
        s_hi, s_lo = sem("s_hi"), sem("s_lo")
        s_pe = sem("s_pe")
        s_silu, s_a, s_ah = sem("s_silu"), sem("s_a"), sem("s_ah")
        s_act, s_u21 = sem("s_act"), sem("s_u21")
        s_braw = [sem("s_braw0"), sem("s_braw1")]
        s_bh, s_bl = sem("s_bh"), sem("s_bl")
        s_ar, s_lh, s_ll = sem("s_ar"), sem("s_lh"), sem("s_ll")
        s_t, s_th, s_tl = sem("s_t"), sem("s_th"), sem("s_tl")
        s_z = sem("s_z")
        s_ya, s_yd = sem("s_ya"), sem("s_yd")
        s_yst = sem("s_yst")
        s_lt, s_lc, s_lg, s_L = sem("s_lt"), sem("s_lc"), sem("s_lg"), sem("s_L")
        s_x0 = sem("s_x0")
        s_v = sem("s_v")
        s_m = sem("s_m")
        s_rk = sem("s_rk")
        s_oh, s_pm, s_meta = sem("s_oh"), sem("s_pm"), sem("s_meta")
        s_b0, s_bd, s_bias = sem("s_b0"), sem("s_bd"), sem("s_bias")
        s_gd = [sem(f"s_gd{i}") for i in range(3)]
        s_tp, s_tc, s_tlo = sem("s_tp"), sem("s_tc"), sem("s_tlo")
        s_blk, s_zr, s_sc = sem("s_blk"), sem("s_zr"), sem("s_sc")

        y_d = nc.dram_tensor("y_scratch", (T, H), F32).ap()

        tok1 = cf[:, 0:16]
        io8 = cf[:, 16:24]
        io40 = cf[:, 24:64]
        thr = cf[:, 64:80]
        tri = cf[:, 80:144]
        io128 = cf[:, 144:272]
        dump = cf[:, 272:273]
        ecol = cf[:, 273:274]
        pcol = cf[:, 274:275]
        cB = ci[:, 0:22]
        cD = ci[:, 22:24]

        block = ctx.enter_context(nc.Block())

        @block.sync
        def _(sp):
            def load(i):
                kind, a, b = pieces[i]
                if i >= RW:
                    sp.wait_ge(s_lo, i - RW + 1)
                if kind == "x":
                    src = xp[a * 4 + b]
                elif kind == "w":
                    src = wp[b]
                else:
                    src = we[a, b]
                sp.dma_start(raw[:, i % RW, :], src).then_inc(s_raw[i % RW], 16)

            load(0)
            load(1)
            sp.dma_start(lorai[:, :], itok.partition_broadcast(128)).then_inc(s_c, 16)
            sp.dma_start(ci[:, :], cst_i).then_inc(s_c, 16)
            load(2)
            for dst, src in ((ident[:, :], ident_d), (ut[:, :], ut_d), (cf[:, :], cst_f), (wg_s[:, :, :], wgt),
                             (bg_s[:, :], bg.partition_broadcast(128))):
                sp.dma_start(dst, src).then_inc(s_cb, 16)
            for i in range(RW, len(pieces)):
                load(i)

        pool = Jobs()

        def ioa(ap):
            return bass.IndirectOffsetOnAxis(ap=ap, axis=0)

        def gather_a(e, g):
            if g == 0:
                e.wait_ge(s_idx, 3)
            else:
                e.wait_ge(s_ll, 2 * g)
            for b in range(2):
                e.indirect_dma_start(out=araw[:, b, :], out_offset=None, in_=agu,
                                     in_offset=ioa(idx_a[:, 2 * g + b:2 * g + b + 1])).then_inc(s_ar, 16)

        def gather_b(e, g, i):
            n = g * 26 + i
            if n >= 2:
                e.wait_ge(s_bl, n - 1)
            if i < NC:
                for b in range(2):
                    e.indirect_dma_start(out=braw[:, n % 2, b * 256:(b + 1) * 256], out_offset=None, in_=bgu,
                                         in_offset=ioa(idx_b[0:96, 2 * g + b, i:i + 1])).then_inc(s_braw[n % 2], 16)
            else:
                h, b = divmod(i - NC, 2)
                e.indirect_dma_start(out=braw[:, n % 2, :], out_offset=None, in_=bdn,
                                     in_offset=ioa(idx_d[0:96, 2 * g + b, h:h + 1])).then_inc(s_braw[n % 2], 16)

        def braw_value(n):
            return 16 * sum(2 if m % 26 < NC else 1 for m in range(n % 2, n + 1, 2))

        def b_use(g, i):
            if i < NC:
                return unit_up(g, i)
            return unit_down(g, (i - NC) // 2, 10)

        def store_y(e, g):
            e.wait_ge(s_ya, 4 * (g + 1))
            e.wait_ge(s_yd, 4 * (g + 1))
            e.dma_start(y_d[g * 512:(g + 1) * 512, :].rearrange("(t p) n -> p t n", p=128),
                        ybuf[:, :, :]).then_inc(s_yst, 16)

        def copy_x(e, g):
            e.dma_start(out[g * 512:(g + 1) * 512, :], xn[g * 512:(g + 1) * 512, :]).then_inc(s_x0, 16)
            if g == 0:
                e.dma_start(out[T:T + 128, :], xn[0:128, :]).then_inc(s_x0, 16)

        for g in range(NG):
            pool.add(g * NU - 30, gather_a, g)
            for i in range(26):
                n = g * 26 + i
                p2 = n - 2
                pool.add(b_use(p2 // 26, p2 % 26) - 6 if n >= 2 else -20, gather_b, g, i)
            pool.add(g * NU + 10, lambda e, g=g: (e.wait_ge(s_pe, g * NU + 6), copy_x(e, g)))
            pool.add(g * NU + NU - 0.5, store_y, g)

        def gather_y(e, b):
            if b == 0:
                e.wait_ge(s_yst, 16 * NG)
                e.wait_ge(s_pm, 2)
                e.wait_ge(s_x0, 16 * (NG + 1))
                e.wait_ge(s_lt, 32)
            if b >= 3:
                e.wait_ge(s_tp, b - 2)
            e.indirect_dma_start(out=ybuf[:, b % 3, :], out_offset=None, in_=y_d,
                                 in_offset=ioa(gidx[:, b:b + 1])).then_inc(s_gd[b % 3], 16)

        def y_lo(e, b):
            e.wait_ge(s_tc, b + 1)
            e.tensor_tensor(ring_t(b % 2, 1), ytp[:, :], ring_t(b % 2, 0), ALU.subtract).then_inc(s_tlo, 1)

        def scatter(e, b):
            e.wait_ge(s_zr, b + 1)
            if b:
                e.wait_ge(s_sc, 16 * b)
            e.indirect_dma_start(out=out, out_offset=ioa(sidx[:, b:b + 1]),
                                 in_=sbuf2[:, 2 * (b % 2):2 * (b % 2) + 2, :].rearrange("p a n -> p (a n)"),
                                 in_offset=None, compute_op=ALU.add).then_inc(s_sc, 16)

        act = Jobs()
        dve = Jobs()

        def arrived(e, i):
            e.wait_ge(s_raw[i % RW], 16 * (i // RW + 1))

        def piece_dst(i, part):
            kind, a, b = pieces[i]
            if kind == "x":
                o = XO + part * 4096 + b * 1024
                return R[:, o:o + 1024]
            if kind == "e":
                return s_w_t(a, b, part)
            return ring_t(a * NU + b, part)

        def early_after(e, k):
            j = 8 * e + k - 4
            return unit_down(NG - 1, 1, j) if j >= 0 else unit_up(NG - 1, NC - 1)

        def split_hi(e, i):
            kind, a, b = pieces[i]
            arrived(e, i)
            if kind == "w":
                n = a * NU + b
                if n >= RW:
                    e.wait_ge(s_pe, n - RW + 1)
            elif kind == "e":
                e.wait_ge(s_pe, early_after(a, b) + 1)
            elif a > 0:
                e.wait_ge(s_pe, (a - 1) * NU + S2)
            e.activation(piece_dst(i, 0), raw[:, i % RW, :], ACT.Copy).then_inc(s_hi, 1)

        def split_lo(e, i):
            e.wait_ge(s_hi, i + 1)
            e.tensor_tensor(piece_dst(i, 1), raw[:, i % RW, :], piece_dst(i, 0), ALU.subtract).then_inc(s_lo, 1)

        for i, (kind, a, b) in enumerate(pieces):
            if kind == "w":
                key = a * NU + b - RW if (a, b) != (0, 0) else -7
            elif kind == "x":
                key = -6 + i * 0.01 if a == 0 else (a - 1) * NU + XAT[b] - RW - 0.1
            elif (a, b) in EARLY:
                key = (NG - 1) * NU + EARLY[a, b] - RW - 0.1
            else:
                break
            act.add(key + 0.5, split_hi, i)
            dve.add(key + 0.55, split_lo, i)

        def grp(ap, off):
            return ap[:, 0:38 * 32].rearrange("p (q m) -> p q m", m=32)[:, :, off:off + 16]

        def a_hi(e, g):
            e.wait_ge(s_ar, 32 * (g + 1))
            e.wait_ge(s_init, 1)
            if g:
                e.wait_ge(s_pe, unit_down(g - 1, 0, 1) + 1)
            for b in range(2):
                e.activation(grp(a_t(b), 0), araw[:, b, :].rearrange("p (q m) -> p q m", m=16),
                             ACT.Copy).then_inc(s_lh, 1)

        def a_lo(e, g):
            for b in range(2):
                e.wait_ge(s_lh, 2 * g + b + 1)
                e.tensor_tensor(grp(a_t(b), 16), araw[:, b, :].rearrange("p (q m) -> p q m", m=16),
                                grp(a_t(b), 0), ALU.subtract).then_inc(s_ll, 1)

        def b_hi(e, n):
            e.wait_ge(s_braw[n % 2], braw_value(n))
            if n >= 2:
                e.wait_ge(s_pe, b_use((n - 2) // 26, (n - 2) % 26) + 1)
            e.activation(b_t(n % 2), braw[:, n % 2, :], ACT.Copy).then_inc(s_bh, 1)

        def b_lo(e, n):
            e.wait_ge(s_bh, n + 1)
            m = b_t(n % 2)[32:64, :]
            e.tensor_tensor(m, braw[32:64, n % 2, :], m, ALU.subtract).then_inc(s_bl, 1)

        def t_hi(e, g):
            e.wait_ge(s_t, 2 * g + 1)
            for q in range(2):
                for r in range(2):
                    e.activation(TT[32 * r:32 * r + 32, q, :], PS[32 * q:32 * q + 32, 2, :], ACT.Copy,
                                 scale=0.5).then_inc(s_th, 1)

        def t_lo(e, g):
            e.wait_ge(s_th, 6 * g + 4)
            for q in range(2):
                e.scalar_tensor_tensor(out=TT[64:96, q, :], in0=PS[32 * q:32 * q + 32, 2, :], scalar=0.5,
                                       in1=TT[0:32, q, :], op0=ALU.mult, op1=ALU.subtract).then_inc(s_tl, 1)

        def td_hi(e, g):
            e.wait_ge(s_t, 2 * g + 2)
            for r in range(2):
                e.activation(TT[32 * r:32 * r + 32, 2, :], PS[0:32, 4, :], ACT.Copy, scale=0.5).then_inc(s_th, 1)

        def td_lo(e, g):
            e.wait_ge(s_th, 6 * g + 6)
            e.scalar_tensor_tensor(out=TT[64:96, 2, :], in0=PS[0:32, 4, :], scalar=0.5, in1=TT[0:32, 2, :],
                                   op0=ALU.mult, op1=ALU.subtract).then_inc(s_tl, 1)

        def silu(e, g, c):
            n = g * NC + c
            e.wait_ge(s_pe, unit_gate(g, c) + 1)
            if n >= 2:
                e.wait_ge(s_a, n - 1)
            bank = 2 * (c % 2)
            if c < NC - 1:
                e.activation(sbuf2[:, c % 2, :], PS[:, bank, :], ACT.Silu).then_inc(s_silu, 1)
            else:
                e.wait_ge(s_act, n)
                e.activation(sbuf2[0:64, c % 2, :], PS[0:64, bank, :], ACT.Silu).then_inc(s_silu, 1)
                e.activation(sbuf2[0:64, 2, :], PS[64:128, bank, :], ACT.Copy).then_inc(s_u21, 1)

        def gated(e, g, c):
            n = g * NC + c
            e.wait_ge(s_silu, n + 1)
            if n >= 2:
                e.wait_ge(s_act, n - 1)
            if c < NC - 1:
                e.wait_ge(s_pe, unit_up(g, c) + 1)
                e.tensor_tensor(sbuf2[:, 2 + c % 2, :], sbuf2[:, c % 2, :], PS[:, 2 * (c % 2) + 1, :],
                                ALU.mult).then_inc(s_a, 1)
            else:
                e.wait_ge(s_u21, g + 1)
                e.tensor_tensor(sbuf2[0:64, 2 + c % 2, :], sbuf2[0:64, c % 2, :], sbuf2[0:64, 2, :],
                                ALU.mult).then_inc(s_a, 1)

        def act_hi(e, g, c):
            n = g * NC + c
            e.wait_ge(s_a, n + 1)
            p = 128 if c < NC - 1 else 64
            e.activation(act_t(c, 0)[0:p, :], sbuf2[0:p, 2 + c % 2, :], ACT.Copy).then_inc(s_ah, 1)

        def act_lo(e, g, c):
            n = g * NC + c
            e.wait_ge(s_ah, n + 1)
            if c < NC - 1:
                dst, p = act_t(c, 1), 128
            else:
                dst, p = act_t(c, 0)[64:128, :], 64
            e.tensor_tensor(dst, sbuf2[0:p, 2 + c % 2, :], act_t(c, 0)[0:p, :], ALU.subtract).then_inc(s_act, 1)

        def y_out(e, g, h, tt, s):
            if tt < 3:
                e.wait_ge(s_z, g * 6 + h * 3 + tt + 1)
            else:
                e.wait_ge(s_pe, unit_down(g, h, 10) + 1)
            if g and h == 0:
                e.wait_ge(s_yst, 16 * g)
                e.wait_ge(s_lt, 8 * g)
            dst = ybuf[:, tt, h * 512:(h + 1) * 512]
            if s is s_ya:
                e.activation(dst, PS[:, 4 * h + tt, :], ACT.Copy).then_inc(s, 1)
            else:
                e.tensor_copy(dst, PS[:, 4 * h + tt, :]).then_inc(s, 1)

        def lt_banks(q):
            return ((5, 6), 7) if q < 12 else ((0, 1), 2 + q % 4 // 2)

        def lt_copy(e, m):
            q, h, slot = LT[m]
            e.wait_ge(s_lt, m + 1)
            if m >= 2:
                e.wait_ge(s_lg, m - 1)
            e.activation(ytp[:, slot * 512:(slot + 1) * 512], PS[:, lt_banks(q)[0][slot], :], ACT.Copy).then_inc(s_lc, 1)

        def l_add(e, q):
            e.wait_ge(s_lg, LT_AT[q if q < 12 else q | 1, 1] + 1)
            if q == 0:
                e.wait_ge(s_cb, 80)
            col = 8 * (q % 4)
            e.tensor_tensor(Lg[:, q, :], PS[:, lt_banks(q)[1], col:col + 8], bg_s[:, :], ALU.add).then_inc(s_L, 1)
            e.wait_ge(s_L, 3 * q + 1)
            e.max(mx[:, q, :], Lg[:, q, :]).then_inc(s_L, 1)
            e.wait_ge(s_L, 3 * q + 2)
            e.max_index(mi[:, q, :], mx[:, q, :], Lg[:, q, :]).then_inc(s_L, 1)

        for g in range(NG):
            a_key = -4.0 if g == 0 else unit_down(g - 1, 0, 3)
            act.add(a_key, a_hi, g)
            dve.add(a_key, a_lo, g)
            act.add(g * NU - 0.25, t_hi, g)
            dve.add(g * NU - 0.24, t_lo, g)
            act.add(unit_down(g, 0, 0) + 0.6, td_hi, g)
            dve.add(unit_down(g, 0, 0) + 0.61, td_lo, g)
            for i in range(26):
                n = g * 26 + i
                key = -0.45 + 0.01 * n if n < 2 else b_use((n - 2) // 26, (n - 2) % 26) + 0.7
                act.add(key, b_hi, n)
                dve.add(key + 0.01, b_lo, n)
            for c in range(NC):
                act.add(unit_gate(g, c) + 0.1, silu, g, c)
                dve.add(unit_up(g, c) + 0.2, gated, g, c)
                act.add(unit_up(g, c) + 0.3, act_hi, g, c)
                dve.add(unit_up(g, c) + 0.4, act_lo, g, c)
            for h in range(2):
                for tt in range(4):
                    (dve if tt % 2 else act).add(unit_down(g, h, 10) + 0.2, y_out, g, h, tt, s_yd if tt % 2 else s_ya)
            for tt in range(4):
                q = 4 * g + tt
                if g < NG - 1:
                    for h in range(2):
                        act.add(unit_gate(g + 1, tt + 1) + 0.06, lt_copy, LT_AT[q, h])
                    dve.add(unit_up(g + 1, tt + 1) + 0.06, l_add, q)
                else:
                    act.add(unit_down(g, 1, tt + 1) + 0.06, lt_copy, LT_AT[q, 0])
                    act.add(unit_down(g, 1, 10) + 0.2, lt_copy, LT_AT[q, 1])
                    dve.add(unit_down(g, 1, 10) + 0.3, l_add, q)

        bias_raw = araw[:, :, :].rearrange("p b n -> p (b n)")[:, 0:1024]
        bias = R[:, 32768:33792]

        def load_bias(e):
            e.wait_ge(s_ll, 2 * NG)
            e.memset(bias_raw, 0.0).then_inc(s_b0, 1)
            e.wait_ge(s_b0, 1)
            e.dma_start(bias_raw[0:8, :], be).then_inc(s_bd, 16)
            e.dma_start(bias_raw[32:40, :], be).then_inc(s_bd, 16)

        def bias_hi(e):
            e.wait_ge(s_bd, 32)
            e.wait_ge(s_pe, NG * NU)
            e.activation(bias, bias_raw, ACT.Copy).then_inc(s_bias, 1)

        def bias_lo(e):
            e.wait_ge(s_bias, 1)
            e.tensor_tensor(bias[32:64, :], bias_raw[32:64, :], bias[32:64, :], ALU.subtract).then_inc(s_bias, 1)

        pool.add(NG * NU - 8, load_bias)
        act.add(NG * NU + 30, bias_hi)
        dve.add(NG * NU + 30, bias_lo)

        def blk_hi(e, b):
            e.wait_ge(s_tp, b + 1)
            if b >= 2:
                e.wait_ge(s_blk, b)
            if b == 0:
                e.wait_ge(s_pm, 2)
                e.wait_ge(s_meta, 1)
            tp = PS[:, 2 * (b % 2):2 * (b % 2) + 2, :].rearrange("p a n -> p (a n)")
            if b:
                e.wait_ge(s_tlo, b)
            e.activation(ytp[:, :], tp, ACT.Copy)
            e.activation(ring_t(b % 2, 0), tp, ACT.Copy).then_inc(s_tc, 1)

        def blk_out(e, b):
            e.wait_ge(s_blk, b + 2)
            if b >= 2:
                e.wait_ge(s_sc, 16 * (b - 1))
            z = PS[:, 4 + 2 * (b % 2):6 + 2 * (b % 2), :]
            e.activation(sbuf2[:, 2 * (b % 2):2 * (b % 2) + 2, :], z, ACT.Relu, scale=0.5).then_inc(s_zr, 1)

        @block.gpsimd
        def _(e):
            e.memset(R[:, LO:RN].bitcast(F32), 0.0).then_inc(s_init, 1)
            pool.run(e)
            for b in range(3):
                gather_y(e, b)
            y_lo(e, 0)
            for b in range(NB):
                if b + 1 < NB:
                    y_lo(e, b + 1)
                if b + 3 < NB:
                    gather_y(e, b + 3)
                scatter(e, b)
            e.wait_ge(s_sc, 16 * NB)

        @block.scalar
        def _(e):
            act.run(e)
            for b in range(NB):
                blk_hi(e, b)
                if b:
                    blk_out(e, b - 1)
            blk_out(e, NB - 1)

        RT = ytp
        OB = ring[:, 0:32 * NBP].rearrange("p (q b) -> p q b", b=NBP)
        OR = ring[:, 32 * NBP:32 * NBP + 4096].rearrange("p (q r) -> p q r", r=128)

        @block.vector
        def _(e):
            n = [0]

            def link(ins):
                n[0] += 1
                ins.then_inc(s_v, 1)
                e.wait_ge(s_v, n[0])

            e.wait_ge(s_c, 32)
            link(e.tensor_copy(loraf[:, :], lorai[:, :]))
            link(e.scalar_tensor_tensor(out=idx_a[:, :], in0=loraf[:, :], scalar=128.0,
                                        in1=ci[:, 24:25].to_broadcast([128, 8]), op0=ALU.mult, op1=ALU.add))
            l3 = loraf[:, :].rearrange("p (b o) -> p b o", o=1)
            link(e.scalar_tensor_tensor(out=idx_b[:, :, :], in0=l3.to_broadcast([128, 8, NC]), scalar=352.0,
                                        in1=cB.rearrange("p (o c) -> p o c", o=1).to_broadcast([128, 8, NC]),
                                        op0=ALU.mult, op1=ALU.add))
            e.scalar_tensor_tensor(out=idx_d[:, :, :], in0=l3.to_broadcast([128, 8, 2]), scalar=32.0,
                                   in1=cD.rearrange("p (o c) -> p o c", o=1).to_broadcast([128, 8, 2]),
                                   op0=ALU.mult, op1=ALU.add).then_inc(s_idx, 3)
            dve.run(e)

            def bc(ap, shape):
                return ap.to_broadcast(shape)

            idf = RT[:, 0:32].rearrange("p (t s) -> p t s", s=2)
            oh = [RT[:, 32 + 128 * s:160 + 128 * s].rearrange("p (t e) -> p t e", e=8) for s in range(2)]
            e.wait_ge(s_L, 48)
            link(e.tensor_copy(idf, mi[:, :, 0:2]))
            for s in range(2):
                link(e.tensor_tensor(oh[s], bc(io8.rearrange("p (o e) -> p o e", o=1), [128, 16, 8]),
                                     bc(idf[:, :, s:s + 1], [128, 16, 8]), ALU.is_equal))
            e.tensor_tensor(msk[:, :, :], oh[0], oh[1], ALU.add).then_inc(s_m, 1)
            e.wait_ge(s_rk, 1)
            rk = PS[:, 0, 0:136].rearrange("p (t e) -> p t e", e=8)
            cmp1 = RT[:, 288:416].rearrange("p (e j) -> p e j", j=16)
            cmp2 = RT[:, 288:352].rearrange("p (e j) -> p e j", j=8)
            nb, cb, base, ne = (RT[:, 416 + 8 * i:424 + 8 * i] for i in range(4))
            link(e.tensor_copy(ne, rk[:, 16, :]))
            link(e.tensor_tensor(cmp1, bc(ne.rearrange("p (e o) -> p e o", o=1), [128, 8, 16]),
                                 bc(thr.rearrange("p (o j) -> p o j", o=1), [128, 8, 16]), ALU.is_gt))
            link(e.tensor_reduce(nb, cmp1, AX.X, ALU.add))
            link(e.tensor_tensor(cmp2, bc(nb.rearrange("p (o j) -> p o j", o=1), [128, 8, 8]),
                                 tri.rearrange("p (e j) -> p e j", j=8), ALU.mult))
            link(e.tensor_reduce(cb, cmp2, AX.X, ALU.add))
            link(e.tensor_tensor(base, cb, nb, ALU.subtract))
            R2 = RT[:, 448:576].rearrange("p (t e) -> p t e", e=8)
            link(e.scalar_tensor_tensor(out=R2, in0=bc(base.rearrange("p (o e) -> p o e", o=1), [128, 16, 8]),
                                        scalar=128.0, in1=rk[:, 0:16, :], op0=ALU.mult, op1=ALU.add))
            pos = RT[:, 576:608].rearrange("p (t s) -> p t s", s=2)
            for s in range(2):
                link(e.tensor_tensor(oh[s], oh[s], R2, ALU.mult))
                link(e.tensor_reduce(pos[:, :, s], oh[s], AX.X, ALU.add))
            link(e.tensor_copy(posi[:, 0, :], RT[:, 576:608]))
            link(e.tensor_scalar(posi[:, 1, :], posi[:, 0, :], 7, None, ALU.logical_shift_right))
            link(e.tensor_scalar(posi[:, 2, :], posi[:, 0, :], 127, None, ALU.bitwise_and))
            blkf, rf = RT[:, 608:640], RT[:, 640:672]
            link(e.tensor_copy(blkf, posi[:, 1, :]))
            link(e.tensor_copy(rf, posi[:, 2, :]))
            link(e.tensor_tensor(OB, bc(io40.rearrange("p (o b) -> p o b", o=1), [128, 32, NBP]),
                                 bc(blkf.rearrange("p (q o) -> p q o", o=1), [128, 32, NBP]), ALU.is_equal))
            OB4 = OB.rearrange("p (t s) b -> p t (s b)", s=2)
            link(e.tensor_tensor(OB4, OB4, bc(tok1.rearrange("p (t o) -> p t o", o=1), [128, 16, 2 * NBP]), ALU.mult))
            for i in range(4):
                e.tensor_tensor(OR[:, 8 * i:8 * i + 8, :], bc(io128.rearrange("p (o r) -> p o r", o=1), [128, 8, 128]),
                                bc(rf[:, 8 * i:8 * i + 8].rearrange("p (q o) -> p q o", o=1), [128, 8, 128]),
                                ALU.is_equal).then_inc(s_oh, 1)
            eb = RT[:, 672:712]
            cm2 = RT[:, 0:320].rearrange("p (b e) -> p b e", e=8)
            link(e.tensor_tensor(cm2, bc(io40.rearrange("p (b o) -> p b o", o=1), [128, NBP, 8]),
                                 bc(cb.rearrange("p (o e) -> p o e", o=1), [128, NBP, 8]), ALU.is_ge))
            link(e.tensor_reduce(eb, cm2, AX.X, ALU.add))
            link(e.tensor_scalar(eb, eb, 7.0, None, ALU.min))
            link(e.tensor_copy(meta[:, 80:80 + NBP], eb))
            link(e.tensor_scalar(meta[:, 0:NBP], meta[:, 80:80 + NBP], 1, None, ALU.bitwise_and))
            link(e.tensor_scalar(meta[:, NBP:2 * NBP], eb, 8.0, float(NP - 56), ALU.mult, ALU.add))
            link(e.tensor_scalar(meta[:, 120:128], cb, 1.0, None, ALU.add))
            e.tensor_tensor(oE[:, :], eb, ecol.to_broadcast([128, NBP]), ALU.is_equal).then_inc(s_meta, 1)
            e.wait_ge(s_rk, 2)
            pm1, isz = RT[:, 712:752], RT[:, 752:792]
            PM = PS[:, 1, 0:NBP]
            link(e.tensor_scalar(pm1, PM, -1.0, None, ALU.add))
            link(e.tensor_scalar(isz, PM, 0.0, dump, ALU.is_equal, ALU.mult))
            e.tensor_scalar(gidx[:, :], pm1, 0.0, None, ALU.max).then_inc(s_pm, 1)
            e.tensor_tensor(sidx[:, :], pm1, isz, ALU.add).then_inc(s_pm, 1)

            for ex in range(1, NE):
                if ex >= 2:
                    e.wait_ge(s_blk, e.value_load(meta[0:1, 118 + ex:119 + ex], min_val=1, max_val=NB + 1))
                for k in range(8):
                    if (ex, k) in EARLY:
                        continue
                    i = at[("e", ex, k)]
                    arrived(e, i)
                    link(e.tensor_copy(s_w_t(ex, k, 0), raw[:, i % RW, :]))
                    e.tensor_tensor(s_w_t(ex, k, 1), raw[:, i % RW, :], s_w_t(ex, k, 0), ALU.subtract).then_inc(s_lo, 1)


        @block.tensor
        def _(e):
            def mm3(out_, hi, lo, whi, wlo, start, stop=False):
                e.matmul(out_, hi, whi, start=start, stop=False)
                e.matmul(out_, hi, wlo, start=False, stop=False)
                return e.matmul(out_, lo, whi, start=False, stop=stop)

            def lora_in(g):
                e.wait_ge(s_ll, 2 * g + 2)
                for b in range(2):
                    for k in range(8):
                        for part in range(2):
                            m = e.matmul(PS[:, 2, b * 256:(b + 1) * 256], a_t(b)[:, k * 64:k * 64 + 128],
                                         x_t(part, k)[:, b * 256:(b + 1) * 256], start=(k == 0 and part == 0),
                                         stop=(k == 7 and part == 1))
                m.then_inc(s_t, 1)

            def lora_out(g, c, bank, q, last):
                n = g * 26 + c
                e.wait_ge(s_bl, n + 1)
                e.wait_ge(s_tl, 3 * g + 2)
                for b in range(2):
                    o = b * 256 + q * 128
                    m = e.matmul(PS[:, bank, b * 256:(b + 1) * 256], b_t(n % 2)[:, o:o + 128],
                                 TT[:, q, b * 256:(b + 1) * 256], start=False, stop=last and b == 1)
                return m

            def first(g, c, q):
                n = g * NU + 2 * c + q
                bank = 2 * (c % 2) + q
                m0 = g * NC + c
                e.wait_ge(s_lo, at[("w", g, 2 * c + q)] + 1)
                if m0 >= 2:
                    if q == 0:
                        e.wait_ge(s_silu, m0 - 1)
                    else:
                        e.wait_ge(s_a, m0 - 1)
                if c % 2 == 0 and g:
                    e.wait_ge(s_u21, g)
                if c == 0 and g:
                    e.wait_ge(s_ya, 4 * g - 2)
                    e.wait_ge(s_yd, 4 * g - 2)
                w = [ring_t(n, 0), ring_t(n, 1)]
                for k in range(8):
                    sl = slice(k * 128, (k + 1) * 128)
                    if c == 0 and q == 0 and k % 2 == 0:
                        e.wait_ge(s_lo, at[("x", g, k // 2)] + 1)
                    e.matmul(PS[:, bank, :], w[0][:, sl], x_t(0, k), start=(k == 0), stop=False)
                    e.matmul(PS[:, bank, :], w[0][:, sl], x_t(1, k), start=False, stop=False)
                    e.matmul(PS[:, bank, :], w[1][:, sl], x_t(0, k), start=False, stop=False)
                if c == NC - 1:
                    lora_out(g, c, bank, 0, False)
                    lora_out(g, c, bank, 1, True).then_inc(s_pe, 1)
                elif c == 0:
                    if q == 0:
                        lora_in(g)
                    else:
                        lora_out(g, 0, 0, 0, True).then_inc(s_pe, 1)
                        lora_out(g, 0, 1, 1, True).then_inc(s_pe, 1)
                else:
                    lora_out(g, c, bank, q, True).then_inc(s_pe, 1)

            def lora_down_in(g, c):
                e.wait_ge(s_act, g * NC + c + 1)
                if c == 0 and g:
                    e.wait_ge(s_ya, 4 * g)
                for part in range(2 if c < NC - 1 else 1):
                    for b in range(2):
                        m = e.matmul(PS[:, 4, b * 256:(b + 1) * 256], a_t(b)[:, (16 + c) * 32:(16 + c) * 32 + 128],
                                     act_t(c, part)[:, b * 256:(b + 1) * 256],
                                     start=(c == 0 and part == 0 and b == 0), stop=(c == NC - 1),
                                     skip_group_check=True)
                if c == NC - 1:
                    m.then_inc(s_t, 1)

            def down(g, h, j):
                n = unit_down(g, h, j)
                e.wait_ge(s_lo, at[("w", g, n - g * NU)] + 1)
                e.wait_ge(s_act, g * NC + 2 * j + 2 if h == 0 else g * NC + NC)
                if j == 0 and h == 0:
                    e.wait_ge(s_a, g * NC + NC - 1)
                    e.wait_ge(s_u21, g + 1)
                if j == 0 and h == 1:
                    e.wait_ge(s_tl, 3 * g + 3)
                    if g:
                        e.wait_ge(s_lc, 8 * g)
                        e.wait_ge(s_L, 12 * g)
                w = [ring_t(n, 0), ring_t(n, 1)]

                def part(tt, cc):
                    c = 2 * j + cc
                    o = PS[:, 4 * h + tt, :]
                    ts = slice(tt * 128, (tt + 1) * 128)
                    whi, wlo = (x[:, cc * 512:(cc + 1) * 512] for x in w)
                    if c < NC - 1:
                        return mm3(o, act_t(c, 0)[:, ts], act_t(c, 1)[:, ts], whi, wlo, start=(c == 0))
                    e.matmul(o, act_t(c, 0)[:, ts], whi, start=False, stop=False)
                    return e.matmul(o, act_t(c, 0)[:, ts], wlo, start=False, stop=False)

                if j < 10:
                    for cc in range(2):
                        for tt in range(4):
                            m = part(tt, cc)
                    m.then_inc(s_pe, 1)
                    return
                e.wait_ge(s_tl, 3 * g + 3)
                e.wait_ge(s_bl, g * 26 + NC + 2 * h + 2)
                for tt in range(4):
                    if g == NG - 1 and h == 1:
                        if tt >= 2:
                            logit_turn(LT_AT[10 + tt, 1])
                        if tt >= 3:
                            logit_sum(LT_AT[9 + tt, 1])
                    part(tt, 0)
                    part(tt, 1)
                    nb_ = g * 26 + NC + 2 * h + tt // 2
                    e.matmul(PS[:, 4 * h + tt, :], TT[:, 2, tt * 128:(tt + 1) * 128], b_t(nb_ % 2),
                             start=False, stop=True).then_inc(s_z if tt < 3 else s_pe, 1)

            def logit_turn(m):
                q, h, slot = LT[m]
                g, tt = q // 4, q % 4
                if m == 0:
                    e.wait_ge(s_cb, 80)
                if m >= 2:
                    e.wait_ge(s_lc, m - 1)
                if g < NG - 1:
                    e.wait_ge(s_ya, 4 * (g + 1))
                    e.wait_ge(s_yd, 4 * (g + 1))
                else:
                    e.wait_ge(s_yd if tt % 2 else s_ya, 4 * g + 2 * h + tt // 2 + 1)
                for k in range(4):
                    i = e.transpose(PS[:, lt_banks(q)[0][slot], k * 128:(k + 1) * 128],
                                    ybuf[:, tt, h * 512 + k * 128:h * 512 + (k + 1) * 128], ident[:, :])
                i.then_inc(s_lt, 1)

            def logit_sum(m):
                q, h, slot = LT[m]
                e.wait_ge(s_lc, m + 1)
                if q and h == 0 and q <= 12:
                    e.wait_ge(s_L, 3 * q - 2)
                col = 8 * (q % 4)
                for k in range(4):
                    i = e.matmul(PS[:, lt_banks(q)[1], col:col + 8],
                                 ytp[:, slot * 512 + k * 128:slot * 512 + (k + 1) * 128], wg_s[:, 4 * h + k, :],
                                 start=(k == 0 and h == 0 and (q < 12 or q % 2 == 0)), stop=(k == 3 and h == 1),
                                 skip_group_check=True)
                i.then_inc(s_lg, 1)

            for g in range(NG):
                for c in range(NC):
                    first(g, c, 0)
                    if g and 1 <= c <= 4:
                        for h in range(2):
                            logit_turn(LT_AT[4 * (g - 1) + c - 1, h])
                    if c:
                        lora_down_in(g, c - 1)
                    if c < NC - 1:
                        first(g, c, 1)
                    if g and 1 <= c <= 4:
                        for h in range(2):
                            logit_sum(LT_AT[4 * (g - 1) + c - 1, h])
                for h in range(2):
                    for j in range(11):
                        down(g, h, j)
                        if h == 0 and j == 0:
                            lora_down_in(g, NC - 1)
                        if g == NG - 1 and h == 1:
                            if 1 <= j <= 4:
                                logit_turn(LT_AT[11 + j, 0])
                            if 2 <= j <= 5:
                                logit_sum(LT_AT[10 + j, 0])
            last = [LT_AT[12 + t, 1] for t in range(4)]
            logit_turn(last[2])
            logit_sum(last[1])
            logit_turn(last[3])
            logit_sum(last[2])
            logit_sum(last[3])

            e.wait_ge(s_m, 1)
            rk = PS[:, 0, 0:136].rearrange("p (t e) -> p t e", e=8)
            for t in range(16):
                n_ = 16 - t
                e.matmul(rk[:, t + 1:17, :], ut[:, 128:256],
                         msk[:, t:t + 1, :].to_broadcast([128, n_, 8]), start=(t == 0), stop=False,
                         skip_group_check=True)
            e.matmul(rk[:, 0:16, :], ut[:, 0:128], msk[:, :, :], start=False, stop=True,
                     skip_group_check=True).then_inc(s_rk, 1)
            for q in range(32):
                if q % 8 == 0:
                    e.wait_ge(s_oh, q // 8 + 1)
                m = e.matmul(PS[:, 1, 0:NBP], OR[:, q, :], OB[:, q, :], start=(q == 0), stop=(q == 31))
            m.then_inc(s_rk, 1)

            def turn(b):
                e.wait_ge(s_gd[b % 3], 16 * (b // 3 + 1))
                if b >= 2:
                    e.wait_ge(s_tc, b - 1)
                for k in range(8):
                    m = e.transpose(PS[:, 2 * (b % 2) + k // 4, (k % 4) * 128:(k % 4 + 1) * 128],
                                    ybuf[:, b % 3, k * 128:(k + 1) * 128], ident[:, :])
                    if b == 0 and k == 0:
                        m.then_inc(s_blk, 1)
                m.then_inc(s_tp, 1)

            e.wait_ge(s_meta, 1)
            turn(0)
            e.wait_ge(s_bias, 2)
            for b in range(NB):
                if b + 1 < NB:
                    turn(b + 1)
                side = e.value_load(meta[0:1, b:b + 1], min_val=0, max_val=1)
                ready = e.value_load(meta[0:1, NBP + b:NBP + b + 1], min_val=NP - 56, max_val=NP)
                off = e.snap(side * 16384)
                e.wait_ge(s_tc, b + 1)
                e.wait_ge(s_tlo, b + 1)
                e.wait_ge(s_lo, ready)
                if b >= 2:
                    e.wait_ge(s_zr, b - 1)
                for k in range(8):
                    ks = slice(k * 128, (k + 1) * 128)
                    hi, lo = ring_t(b % 2, 0)[:, ks], ring_t(b % 2, 1)[:, ks]
                    for n in range(2):
                        o = PS[:, 4 + 2 * (b % 2) + n, :]
                        w = [R[:, bass.ds(off + (k * 2048 + p * 1024 + n * 512), 512)] for p in range(2)]
                        mm3(o, hi, lo, w[0], w[1], start=(k == 0))
                for n in range(2):
                    m = e.matmul(PS[:, 4 + 2 * (b % 2) + n, :], oE[:, b:b + 1].to_broadcast([128, 128]),
                                 bias[:, n * 512:(n + 1) * 512], start=False, stop=True)
                m.then_inc(s_blk, 1)


def tables():
    import numpy as np

    p = np.arange(128)
    cf = np.zeros((128, 512), np.float32)
    cf[:, 0:16] = 128 * np.arange(16)[None] + p[:, None] + 1
    cf[:, 16:24] = np.arange(8)
    cf[:, 24:64] = np.arange(40)
    cf[:, 64:80] = 128 * np.arange(16)
    cf[:, 80:144] = (np.arange(8)[None, :] <= np.arange(8)[:, None]).reshape(-1)
    cf[:, 144:272] = np.arange(128)
    cf[:, 272] = 2049 + p
    cf[:, 273] = np.where(p < 8, p, np.where((p >= 32) & (p < 40), p - 32, -1))
    ci = np.zeros((128, 32), np.float32)
    ci[:, 0:22] = ((p % 16) * 22)[:, None] + np.arange(22)
    ci[:, 22:24] = ((p % 16) * 2)[:, None] + np.arange(2)
    ci[:, 24] = p
    ut = np.concatenate([(p[:, None] < p[None, :]), np.ones((128, 128), bool)], 1)
    return cf, ci, np.eye(128, dtype=np.float32), ut


def kernel(**inputs):
    import ml_dtypes
    import numpy as np
    import concourse.bacc as bacc
    from concourse import mybir as mb
    from concourse.bass_utils import run_bass_kernel_spmd as run

    A = {k: np.asarray(v) for k, v in inputs.items()}
    x = A["x"].reshape(T, H)
    xp = x.reshape(4, 512, 4, 2, 128).transpose(0, 2, 4, 3, 1).reshape(16, 128, 1024)

    def first(w):
        n = w.shape[0] // 128
        return w.reshape(n, 128, 8, 128).transpose(0, 3, 2, 1).reshape(n, 128, 1024)

    wg, wu, wd = A["L0_cond_W_gate"], A["L0_cond_W_up"], A["L0_cond_W_down"]
    g21, u21 = first(wg[:2688]), first(wu[:2688])
    both = first(np.concatenate([wg[2688:], wu[2688:]], 0))
    wdt = wd.T
    wdt = np.concatenate([wdt, wdt[2688:]], 0)
    dn = wdt.reshape(11, 2, 128, 2, 512).transpose(3, 0, 2, 1, 4).reshape(22, 128, 1024)
    wp = np.concatenate([np.stack([g21, u21], 1).reshape(42, 128, 1024), both, dn], 0)

    ag, au, ad = (A["L0_cond_A_" + n][0] for n in ("gate", "up", "down"))
    agu = np.stack([ag, au], 1).reshape(16, 2, 16, 8, 128).transpose(0, 4, 3, 1, 2).reshape(16, 128, 256)
    adt = np.concatenate([ad, ad[:, :, 2688:]], 2)
    adt = adt.reshape(16, 16, 22, 128).transpose(0, 3, 2, 1).reshape(16, 128, 352)
    at_ = np.concatenate([agu, adt], 2).reshape(2048, 608)

    bgt, but, bdt = (A["L0_cond_B_" + n][0].transpose(0, 2, 1) for n in ("gate", "up", "down"))
    z = np.zeros((16, 16, 64), np.float32)
    bgt = np.concatenate([bgt, z], 2).reshape(16, 16, 22, 1, 128)
    but = np.concatenate([but[:, :, :2688], z, but[:, :, 2688:]], 2).reshape(16, 16, 22, 1, 128)
    bgu = np.concatenate([bgt, but], 3).reshape(16 * 16 * 22, 256)
    bdn = bdt.reshape(16 * 16 * 2, 512)

    wgt = A["L0_ffn_W_gate"].reshape(8, 128, 8).transpose(1, 0, 2)
    we = A["L0_ffn_W_e"].reshape(8, 8, 128, 1024)
    cf, ci, ident, ut = tables()
    arrays = {
        "xp": xp, "xn": x, "wp": wp, "agu": at_, "bgu": bgu, "bdn": bdn,
        "itok": A["itok_B_2_6"], "wgt": wgt, "bg": A["L0_ffn_b_gate"], "we": we, "be": A["L0_ffn_b_e"],
        "cst_f": cf, "cst_i": ci, "ident": ident, "ut": ut.astype(ml_dtypes.bfloat16),
    }
    arrays = {k: np.ascontiguousarray(v) for k, v in arrays.items()}
    nc = bacc.Bacc("TRN2", target_bir_lowering=False, num_devices=1, dynamic_dma_scratch_size=4096)
    args = [nc.dram_tensor(f"in_{k}", v.shape, mb.dt.from_np(v.dtype), kind="ExternalInput").ap()
            for k, v in arrays.items()]
    out = nc.dram_tensor("out_0", (T + 128, H), mb.dt.float32, kind="ExternalOutput").ap()
    build(nc, *args, out)
    r = run(nc, [{f"in_{k}": v for k, v in arrays.items()}], core_ids=[0])
    return r.results[0]["out_0"][:T].reshape(8, 256, 1024)
```

```python
from contextlib import ExitStack

import concourse.bass as bass
from concourse import mybir

F32 = mybir.dt.float32
F32R = mybir.dt.float32r
BF16 = mybir.dt.bfloat16
I32 = mybir.dt.int32
U32 = mybir.dt.uint32
ALU = mybir.AluOpType
ACT = mybir.ActivationFunctionType
AX = mybir.AxisListType

T = 2048
H = 1024
F = 2752
NG = 4
NC = 22
NU = 65
S2 = 43
NE = 8
NB = 39
NBP = 40
RW = 3
XAT = [S2 + 4, S2 + 7, S2 + 10, S2 + 13]


EARLY = {(0, 0): S2 + 3, (0, 1): S2 + 5, (0, 2): S2 + 7, (0, 3): S2 + 9, (0, 4): S2 + 15, (0, 5): S2 + 16,
         (0, 6): S2 + 17, (0, 7): S2 + 18, (1, 0): S2 + 19, (1, 1): S2 + 20, (1, 2): S2 + 21}


class Jobs:

    def __init__(self):
        self.jobs = []

    def add(self, key, fn, *args):
        self.jobs.append((key, len(self.jobs), fn, args))

    def run(self, eng):
        for _, _, fn, args in sorted(self.jobs, key=lambda j: j[:2]):
            fn(eng, *args)


def unit_gate(g, c):
    return g * NU + 2 * c


def unit_up(g, c):
    return g * NU + (2 * c + 1 if c < NC - 1 else 2 * c)


def unit_down(g, h, j):
    return g * NU + S2 + 11 * h + j


def piece_list():
    out = [("w", 0, 0)] + [("x", 0, i) for i in range(4)]
    for g in range(NG):
        for n in range(NU):
            if g + 1 < NG and n in XAT:
                out.append(("x", g + 1, XAT.index(n)))
            if g == NG - 1:
                out += [("e", e, k) for e, k in EARLY if EARLY[e, k] == n]
            if (g, n) != (0, 0):
                out.append(("w", g, n))
    for e in range(NE):
        for k in range(8):
            if (e, k) not in EARLY:
                out.append(("e", e, k))
    return out


def build(nc, xp, xn, wp, agu, bgu, bdn, itok, wgt, wgb, bg, we, be, cst_f, cst_i, ident_d, ut_d, out):
    pieces = piece_list()
    at = {p: i for i, p in enumerate(pieces)}
    LT = [(12 + t, h, t % 2) for h in range(2) for t in range(4)]
    LT_AT = {(q, h): m for m, (q, h, _) in enumerate(LT)}
    NP = len(pieces)

    ctx = ExitStack()
    with ctx:
        def sb(name, shape, dt):
            return ctx.enter_context(nc.sbuf_tensor(name, shape, dt))

        def sem(name):
            return ctx.enter_context(nc.semaphore(name))

        XO, AO = 0, 8192
        BO = AO + 21 * 1024 + 512
        LO = BO + 2 * 512
        LA = 38 * 32 + 96
        RN = LO + 2 * LA
        R = sb("R", [128, RN], F32R)
        ring = sb("ring", [128, RW * 2048], F32R)
        TT = sb("TT", [96, 3, 512], F32R)
        raw = sb("raw", [128, RW, 1024], F32)
        braw = sb("braw", [96, 2, 512], F32)
        araw = sb("araw", [128, 2, 608], F32)
        ybuf = sb("ybuf", [128, 4, 1024], F32)
        sbuf2 = sb("sbuf2", [128, 4, 512], F32)
        ytp = sb("ytp", [128, 1024], F32)
        ident = sb("ident", [128, 128], F32)
        ut = sb("ut", [128, 256], BF16)
        cf = sb("cf", [128, 352], F32)
        ci = sb("ci", [128, 32], F32)
        wg_s = sb("wg_s", [128, 8, 8], F32)
        bg_s = sb("bg_s", [128, 8], F32)
        Lp = sb("Lp", [128, 2, 4, 8], F32)
        Lg = sb("Lg", [128, 16, 8], F32)
        mx = sb("mx", [128, 16, 8], F32)
        mi = sb("mi", [128, 16, 8], U32)
        lorai = sb("lorai", [128, 8], I32)
        loraf = sb("loraf", [128, 8], F32)
        idx_a = sb("idx_a", [128, 8], U32)
        idx_b = sb("idx_b", [128, 8, NC], U32)
        idx_d = sb("idx_d", [128, 8, 2], U32)
        gidx = sb("gidx", [128, NBP], U32)
        sidx = sb("sidx", [128, NBP], U32)
        meta = sb("meta", [128, 128], I32)
        oE = sb("oE", [128, NBP], F32R)
        msk = sb("msk", [128, 16, 8], BF16)
        rf = sb("rf", [128, 32], F32)
        posi = sb("posi", [128, 3, 32], U32)
        PS = ctx.enter_context(nc.psum_tensor("PS", [128, 8, 512], F32))

        def x_t(part, k):
            return R[:, XO + part * 4096 + k * 512: XO + part * 4096 + (k + 1) * 512]

        def act_t(c, part):
            o = AO + c * 1024 + part * 512
            return R[:, o:o + 512]

        def b_t(slot):
            return R[0:96, BO + slot * 512: BO + (slot + 1) * 512]

        def a_t(b):
            return R[:, LO + b * LA: LO + (b + 1) * LA]

        def ring_t(n, part):
            o = (n % RW) * 2048 + part * 1024
            return ring[:, o:o + 1024]

        def s_w_t(e, k, part):
            o = (e % 2) * 16384 + k * 2048 + part * 1024
            return R[:, o:o + 1024]

        s_c = sem("s_c")
        s_cb = sem("s_cb")
        s_init = sem("s_init")
        s_idx = sem("s_idx")
        s_raw = [sem(f"s_raw{i}") for i in range(RW)]
        s_hi, s_lo = sem("s_hi"), sem("s_lo")
        s_pe = sem("s_pe")
        s_silu, s_a, s_ah = sem("s_silu"), sem("s_a"), sem("s_ah")
        s_act, s_u21 = sem("s_act"), sem("s_u21")
        s_braw = [sem("s_braw0"), sem("s_braw1")]
        s_bh, s_bl = sem("s_bh"), sem("s_bl")
        s_ar, s_lh, s_ll = sem("s_ar"), sem("s_lh"), sem("s_ll")
        s_t, s_th, s_tl = sem("s_t"), sem("s_th"), sem("s_tl")
        s_z = sem("s_z")
        s_ya, s_yd = sem("s_ya"), sem("s_yd")
        s_yst = sem("s_yst")
        s_lt, s_lc, s_lg, s_L = sem("s_lt"), sem("s_lc"), sem("s_lg"), sem("s_L")
        s_wb = [sem("s_wb0"), sem("s_wb1")]
        s_lm = sem("s_lm")
        s_x0 = sem("s_x0")
        s_v = sem("s_v")
        s_m = sem("s_m")
        s_rk = sem("s_rk")
        s_oh, s_pm, s_meta = sem("s_oh"), sem("s_pm"), sem("s_meta")
        s_b0, s_bd, s_bias = sem("s_b0"), sem("s_bd"), sem("s_bias")
        s_gd = [sem(f"s_gd{i}") for i in range(3)]
        s_tp, s_tc, s_tlo = sem("s_tp"), sem("s_tc"), sem("s_tlo")
        s_blk, s_zr, s_sc = sem("s_blk"), sem("s_zr"), sem("s_sc")

        y_d = nc.dram_tensor("y_scratch", (T, H), F32).ap()

        tok1 = cf[:, 0:16]
        io8 = cf[:, 16:24]
        io40 = cf[:, 24:64]
        thr = cf[:, 64:80]
        tri = cf[:, 80:208]
        io128 = cf[:, 208:336]
        dump = cf[:, 336:337]
        ecol = cf[:, 337:338]
        cB = ci[:, 0:22]
        cD = ci[:, 22:24]

        block = ctx.enter_context(nc.Block())

        def logit_unit(o):
            return 2 * (o // 3)

        @block.sync
        def _(sp):
            def load(i):
                kind, a, b = pieces[i]
                if i >= RW:
                    sp.wait_ge(s_lo, i - RW + 1)
                if kind == "x":
                    src = xp[a * 4 + b]
                elif kind == "w":
                    src = wp[b]
                else:
                    src = we[a, b]
                sp.dma_start(raw[:, i % RW, :], src).then_inc(s_raw[i % RW], 16)

            def wb_before(n):
                g, s = divmod(n, 16)
                if s < 2:
                    return "w", g, 55 + s
                return "w", g + 1, logit_unit(4 * (s - 2) + 3) + 7

            def load_wb(n):
                if n >= 2:
                    sp.wait_ge(s_lm, 4 * (n - 1))
                sp.dma_start(ytp[:, (n % 2) * 512:(n % 2) * 512 + 512],
                             wgb[n % 16].partition_broadcast(128)).then_inc(s_wb[n % 2], 16)

            load(0)
            load(1)
            sp.dma_start(lorai[:, :], itok.partition_broadcast(128)).then_inc(s_c, 16)
            sp.dma_start(ci[:, :], cst_i).then_inc(s_c, 16)
            load(2)
            for dst, src in ((ident[:, :], ident_d), (ut[:, :], ut_d), (cf[:, :], cst_f), (wg_s[:, :, :], wgt),
                             (bg_s[:, :], bg.partition_broadcast(128))):
                sp.dma_start(dst, src).then_inc(s_cb, 16)
            wb = {}
            for n in range(48):
                wb.setdefault(at[wb_before(n)], []).append(n)
            for i in range(RW, len(pieces)):
                for n in wb.get(i, ()):
                    load_wb(n)
                load(i)

        pool = Jobs()

        def ioa(ap):
            return bass.IndirectOffsetOnAxis(ap=ap, axis=0)

        def gather_a(e, g):
            if g == 0:
                e.wait_ge(s_idx, 3)
            else:
                e.wait_ge(s_ll, 2 * g)
            for b in range(2):
                e.indirect_dma_start(out=araw[:, b, :], out_offset=None, in_=agu,
                                     in_offset=ioa(idx_a[:, 2 * g + b:2 * g + b + 1])).then_inc(s_ar, 16)

        def gather_b(e, g, i):
            n = g * 26 + i
            if n >= 2:
                e.wait_ge(s_bl, n - 1)
            if i < NC:
                for b in range(2):
                    e.indirect_dma_start(out=braw[:, n % 2, b * 256:(b + 1) * 256], out_offset=None, in_=bgu,
                                         in_offset=ioa(idx_b[0:96, 2 * g + b, i:i + 1])).then_inc(s_braw[n % 2], 16)
            else:
                h, b = divmod(i - NC, 2)
                e.indirect_dma_start(out=braw[:, n % 2, :], out_offset=None, in_=bdn,
                                     in_offset=ioa(idx_d[0:96, 2 * g + b, h:h + 1])).then_inc(s_braw[n % 2], 16)

        def braw_value(n):
            return 16 * sum(2 if m % 26 < NC else 1 for m in range(n % 2, n + 1, 2))

        def b_use(g, i):
            if i < NC:
                return unit_up(g, i)
            return unit_down(g, (i - NC) // 2, 10)

        def store_y(e, g, h, t0, t1):
            e.wait_ge(s_ya, 4 * g + 2 * h + (t1 + 1) // 2)
            e.wait_ge(s_yd, 4 * g + 2 * h + t1 // 2)
            cols = slice(h * 512, (h + 1) * 512)
            e.dma_start(y_d[g * 512 + t0 * 128:g * 512 + t1 * 128, cols].rearrange("(t p) n -> p t n", p=128),
                        ybuf[:, t0:t1, cols]).then_inc(s_yst, 16)

        def copy_x(e, g):
            e.dma_start(out[g * 512:(g + 1) * 512, :], xn[g * 512:(g + 1) * 512, :]).then_inc(s_x0, 16)
            if g == 0:
                e.dma_start(out[T:T + 128, :], xn[0:128, :]).then_inc(s_x0, 16)

        for g in range(NG):
            pool.add(g * NU - 30, gather_a, g)
            for i in range(26):
                n = g * 26 + i
                p2 = n - 2
                pool.add(b_use(p2 // 26, p2 % 26) - 6 if n >= 2 else -20, gather_b, g, i)
            pool.add(g * NU + 10, lambda e, g=g: (e.wait_ge(s_pe, g * NU + 6), copy_x(e, g)))
            pool.add(g * NU + NU - 11, store_y, g, 0, 0, 4)
            if g < NG - 1:
                pool.add(g * NU + NU - 0.5, store_y, g, 1, 0, 4)
            else:
                for t in range(4):
                    pool.add(g * NU + NU - 0.5, store_y, g, 1, t, t + 1)

        def gather_y(e, b):
            if b == 0:
                e.wait_ge(s_yst, 16 * (2 * NG + 3))
                e.wait_ge(s_pm, 2)
                e.wait_ge(s_x0, 16 * (NG + 1))
                e.wait_ge(s_lt, 8)
            if b >= 3:
                e.wait_ge(s_tp, b - 2)
            e.indirect_dma_start(out=ybuf[:, b % 3, :], out_offset=None, in_=y_d,
                                 in_offset=ioa(gidx[:, b:b + 1])).then_inc(s_gd[b % 3], 16)

        def y_lo(e, b):
            e.wait_ge(s_tc, b + 1)
            e.tensor_tensor(ring_t(b % 2, 1), ytp[:, :], ring_t(b % 2, 0), ALU.subtract).then_inc(s_tlo, 1)

        def scatter(e, b):
            e.wait_ge(s_zr, b + 1)
            if b:
                e.wait_ge(s_sc, 16 * b)
            e.indirect_dma_start(out=out, out_offset=ioa(sidx[:, b:b + 1]),
                                 in_=sbuf2[:, 2 * (b % 2):2 * (b % 2) + 2, :].rearrange("p a n -> p (a n)"),
                                 in_offset=None, compute_op=ALU.add).then_inc(s_sc, 16)

        act = Jobs()
        dve = Jobs()

        def arrived(e, i):
            e.wait_ge(s_raw[i % RW], 16 * (i // RW + 1))

        def piece_dst(i, part):
            kind, a, b = pieces[i]
            if kind == "x":
                o = XO + part * 4096 + b * 1024
                return R[:, o:o + 1024]
            if kind == "e":
                return s_w_t(a, b, part)
            return ring_t(a * NU + b, part)

        def early_after(e, k):
            j = 8 * e + k - 4
            return unit_down(NG - 1, 1, j) if j >= 0 else unit_up(NG - 1, NC - 1)

        def split_hi(e, i):
            kind, a, b = pieces[i]
            arrived(e, i)
            if kind == "w":
                n = a * NU + b
                if n >= RW:
                    e.wait_ge(s_pe, n - RW + 1)
            elif kind == "e":
                e.wait_ge(s_pe, early_after(a, b) + 1)
            elif a > 0:
                e.wait_ge(s_pe, (a - 1) * NU + S2)
            e.activation(piece_dst(i, 0), raw[:, i % RW, :], ACT.Copy).then_inc(s_hi, 1)

        def split_lo(e, i):
            e.wait_ge(s_hi, i + 1)
            e.tensor_tensor(piece_dst(i, 1), raw[:, i % RW, :], piece_dst(i, 0), ALU.subtract).then_inc(s_lo, 1)

        for i, (kind, a, b) in enumerate(pieces):
            if kind == "w":
                key = a * NU + b - RW if (a, b) != (0, 0) else -7
            elif kind == "x":
                key = -6 + i * 0.01 if a == 0 else (a - 1) * NU + XAT[b] - RW - 0.1
            elif (a, b) in EARLY:
                key = (NG - 1) * NU + EARLY[a, b] - RW - 0.1
            else:
                break
            act.add(key + 0.5, split_hi, i)
            dve.add(key + 0.55, split_lo, i)

        def grp(ap, off):
            return ap[:, 0:38 * 32].rearrange("p (q m) -> p q m", m=32)[:, :, off:off + 16]

        def a_hi(e, g):
            e.wait_ge(s_ar, 32 * (g + 1))
            e.wait_ge(s_init, 1)
            if g:
                e.wait_ge(s_pe, unit_down(g - 1, 0, 1) + 1)
            for b in range(2):
                e.activation(grp(a_t(b), 0), araw[:, b, :].rearrange("p (q m) -> p q m", m=16),
                             ACT.Copy).then_inc(s_lh, 1)

        def a_lo(e, g):
            for b in range(2):
                e.wait_ge(s_lh, 2 * g + b + 1)
                e.tensor_tensor(grp(a_t(b), 16), araw[:, b, :].rearrange("p (q m) -> p q m", m=16),
                                grp(a_t(b), 0), ALU.subtract).then_inc(s_ll, 1)

        def b_hi(e, n):
            e.wait_ge(s_braw[n % 2], braw_value(n))
            if n >= 2:
                e.wait_ge(s_pe, b_use((n - 2) // 26, (n - 2) % 26) + 1)
            e.activation(b_t(n % 2), braw[:, n % 2, :], ACT.Copy).then_inc(s_bh, 1)

        def b_lo(e, n):
            e.wait_ge(s_bh, n + 1)
            m = b_t(n % 2)[32:64, :]
            e.tensor_tensor(m, braw[32:64, n % 2, :], m, ALU.subtract).then_inc(s_bl, 1)

        def t_hi(e, g):
            e.wait_ge(s_t, 2 * g + 1)
            for q in range(2):
                for r in range(2):
                    e.activation(TT[32 * r:32 * r + 32, q, :], PS[32 * q:32 * q + 32, 2, :], ACT.Copy,
                                 scale=0.5).then_inc(s_th, 1)

        def t_lo(e, g):
            e.wait_ge(s_th, 6 * g + 4)
            for q in range(2):
                e.scalar_tensor_tensor(out=TT[64:96, q, :], in0=PS[32 * q:32 * q + 32, 2, :], scalar=0.5,
                                       in1=TT[0:32, q, :], op0=ALU.mult, op1=ALU.subtract).then_inc(s_tl, 1)

        def td_hi(e, g):
            e.wait_ge(s_t, 2 * g + 2)
            for r in range(2):
                e.activation(TT[32 * r:32 * r + 32, 2, :], PS[0:32, 4, :], ACT.Copy, scale=0.5).then_inc(s_th, 1)

        def td_lo(e, g):
            e.wait_ge(s_th, 6 * g + 6)
            e.scalar_tensor_tensor(out=TT[64:96, 2, :], in0=PS[0:32, 4, :], scalar=0.5, in1=TT[0:32, 2, :],
                                   op0=ALU.mult, op1=ALU.subtract).then_inc(s_tl, 1)

        def silu(e, g, c):
            n = g * NC + c
            e.wait_ge(s_pe, unit_gate(g, c) + 1)
            if n >= 2:
                e.wait_ge(s_a, n - 1)
            bank = 2 * (c % 2)
            if c < NC - 1:
                e.activation(sbuf2[:, c % 2, :], PS[:, bank, :], ACT.Silu).then_inc(s_silu, 1)
            else:
                e.wait_ge(s_act, n)
                e.activation(sbuf2[0:64, c % 2, :], PS[0:64, bank, :], ACT.Silu).then_inc(s_silu, 1)
                e.activation(sbuf2[0:64, 2, :], PS[64:128, bank, :], ACT.Copy).then_inc(s_u21, 1)

        def gated(e, g, c):
            n = g * NC + c
            e.wait_ge(s_silu, n + 1)
            if n >= 2:
                e.wait_ge(s_act, n - 1)
            if c < NC - 1:
                e.wait_ge(s_pe, unit_up(g, c) + 1)
                e.tensor_tensor(sbuf2[:, 2 + c % 2, :], sbuf2[:, c % 2, :], PS[:, 2 * (c % 2) + 1, :],
                                ALU.mult).then_inc(s_a, 1)
            else:
                e.wait_ge(s_u21, g + 1)
                e.tensor_tensor(sbuf2[0:64, 2 + c % 2, :], sbuf2[0:64, c % 2, :], sbuf2[0:64, 2, :],
                                ALU.mult).then_inc(s_a, 1)

        def act_hi(e, g, c):
            n = g * NC + c
            e.wait_ge(s_a, n + 1)
            p = 128 if c < NC - 1 else 64
            e.activation(act_t(c, 0)[0:p, :], sbuf2[0:p, 2 + c % 2, :], ACT.Copy).then_inc(s_ah, 1)

        def act_lo(e, g, c):
            n = g * NC + c
            e.wait_ge(s_ah, n + 1)
            if c < NC - 1:
                dst, p = act_t(c, 1), 128
            else:
                dst, p = act_t(c, 0)[64:128, :], 64
            e.tensor_tensor(dst, sbuf2[0:p, 2 + c % 2, :], act_t(c, 0)[0:p, :], ALU.subtract).then_inc(s_act, 1)

        def y_out(e, g, h, tt, s):
            if tt < 3:
                e.wait_ge(s_z, g * 6 + h * 3 + tt + 1)
            else:
                e.wait_ge(s_pe, unit_down(g, h, 10) + 1)
            if g and h == 0:
                e.wait_ge(s_yst, 32 * g)
                e.wait_ge(s_lm, 64 * g)
            dst = ybuf[:, tt, h * 512:(h + 1) * 512]
            if s is s_ya:
                e.activation(dst, PS[:, 4 * h + tt, :], ACT.Copy).then_inc(s, 1)
            else:
                e.tensor_copy(dst, PS[:, 4 * h + tt, :]).then_inc(s, 1)

        def lt_copy(e, m):
            q, h, slot = LT[m]
            e.wait_ge(s_lt, m + 1)
            if m >= 2:
                e.wait_ge(s_lg, m - 1)
            e.activation(ytp[:, slot * 512:(slot + 1) * 512], PS[:, slot, :], ACT.Copy).then_inc(s_lc, 1)

        def best(e, q, t, n):
            e.wait_ge(s_L, n)
            for r in range(q, q + t):
                m = e.max(mx[:, r, :], Lg[:, r, :])
            m.then_inc(s_L, 1)
            e.wait_ge(s_L, n + 1)
            for r in range(q, q + t):
                m = e.max_index(mi[:, r, :], mx[:, r, :], Lg[:, r, :])
            m.then_inc(s_L, 1)

        def l_step(e, g, o):
            s, tt = divmod(o, 4)
            h, x = divmod(s, 8)
            n = 64 * g + o
            if o == 0:
                e.wait_ge(s_ya, 4 * (g + 1))
                e.wait_ge(s_yd, 4 * (g + 1))
            if tt == 0:
                e.wait_ge(s_wb[s % 2], 16 * (8 * g + s // 2 + 1))
            if n >= 3:
                e.wait_ge(s_lm, n - 2)
            e.tensor_tensor_reduce(out=PS[:, 5 + n % 3, :], in0=ybuf[:, tt, h * 512:(h + 1) * 512],
                                   in1=ytp[:, (s % 2) * 512:(s % 2) * 512 + 512], scale=1.0, scalar=0.0,
                                   op0=ALU.mult, op1=ALU.add, accum_out=Lp[:, h, tt, x:x + 1]).then_inc(s_lm, 1)

        def l_sum(e, g):
            e.wait_ge(s_lm, 64 * (g + 1))
            if g == 0:
                e.wait_ge(s_cb, 80)
            lg = Lg[:, 4 * g:4 * g + 4, :]
            e.tensor_tensor(lg, Lp[:, 0], Lp[:, 1], ALU.add).then_inc(s_L, 1)
            e.wait_ge(s_L, 4 * g + 1)
            e.tensor_tensor(lg, lg, bg_s[:, :].rearrange("p (o b) -> p o b", o=1).to_broadcast([128, 4, 8]),
                            ALU.add).then_inc(s_L, 1)
            best(e, 4 * g, 4, 4 * g + 2)

        def l_add(e, q):
            e.wait_ge(s_lg, LT_AT[q + 1, 1] + 1)
            n = 12 + 3 * ((q - 12) // 2)
            col = 8 * (q % 4)
            e.tensor_tensor(Lg[:, q:q + 2, :],
                            PS[:, 2 + (q - 12) // 2, col:col + 16].rearrange("p (a b) -> p a b", b=8),
                            bg_s[:, :].rearrange("p (o b) -> p o b", o=1).to_broadcast([128, 2, 8]),
                            ALU.add).then_inc(s_L, 1)
            best(e, q, 2, n + 1)

        for g in range(NG):
            a_key = -4.0 if g == 0 else unit_down(g - 1, 0, 3)
            act.add(a_key, a_hi, g)
            dve.add(a_key, a_lo, g)
            act.add(g * NU - 0.25, t_hi, g)
            dve.add(g * NU - 0.24, t_lo, g)
            act.add(unit_down(g, 0, 0) + 0.6, td_hi, g)
            dve.add(unit_down(g, 0, 0) + 0.61, td_lo, g)
            for i in range(26):
                n = g * 26 + i
                key = -0.45 + 0.01 * n if n < 2 else b_use((n - 2) // 26, (n - 2) % 26) + 0.7
                act.add(key, b_hi, n)
                dve.add(key + 0.01, b_lo, n)
            for c in range(NC):
                act.add(unit_gate(g, c) + 0.1, silu, g, c)
                dve.add(unit_up(g, c) + 0.2, gated, g, c)
                act.add(unit_up(g, c) + 0.3, act_hi, g, c)
                dve.add(unit_up(g, c) + 0.4, act_lo, g, c)
            for h in range(2):
                for tt in range(4):
                    (dve if tt % 2 else act).add(unit_down(g, h, 10) + 0.2, y_out, g, h, tt, s_yd if tt % 2 else s_ya)
            if g < NG - 1:
                for o in range(64):
                    dve.add((g + 1) * NU + logit_unit(o) + 0.6, l_step, g, o)
                dve.add((g + 1) * NU + logit_unit(63) + 0.65, l_sum, g)
        for q in range(12, 16):
            act.add(unit_down(NG - 1, 1, q - 11) + 0.06, lt_copy, LT_AT[q, 0])
            act.add(unit_down(NG - 1, 1, 10) + 0.2, lt_copy, LT_AT[q, 1])
            if q % 2:
                dve.add(unit_down(NG - 1, 1, 10) + 0.3, l_add, q - 1)

        bias_raw = araw[:, :, :].rearrange("p b n -> p (b n)")[:, 0:1024]
        bias = R[:, 32768:33792]

        def load_bias(e):
            e.wait_ge(s_ll, 2 * NG)
            e.memset(bias_raw, 0.0).then_inc(s_b0, 1)
            e.wait_ge(s_b0, 1)
            e.dma_start(bias_raw[0:8, :], be).then_inc(s_bd, 16)
            e.dma_start(bias_raw[32:40, :], be).then_inc(s_bd, 16)

        def bias_hi(e):
            e.wait_ge(s_bd, 32)
            e.wait_ge(s_pe, NG * NU)
            e.activation(bias, bias_raw, ACT.Copy).then_inc(s_bias, 1)

        def bias_lo(e):
            e.wait_ge(s_bias, 1)
            e.tensor_tensor(bias[32:64, :], bias_raw[32:64, :], bias[32:64, :], ALU.subtract).then_inc(s_bias, 1)

        pool.add(NG * NU - 8, load_bias)
        act.add(NG * NU + 30, bias_hi)
        dve.add(NG * NU + 30, bias_lo)

        def blk_hi(e, b):
            e.wait_ge(s_tp, b + 1)
            if b >= 2:
                e.wait_ge(s_blk, b)
            if b == 0:
                e.wait_ge(s_pm, 2)
                e.wait_ge(s_meta, 1)
            tp = PS[:, 2 * (b % 2):2 * (b % 2) + 2, :].rearrange("p a n -> p (a n)")
            if b:
                e.wait_ge(s_tlo, b)
            e.activation(ytp[:, :], tp, ACT.Copy)
            e.activation(ring_t(b % 2, 0), tp, ACT.Copy).then_inc(s_tc, 1)

        def blk_out(e, b):
            e.wait_ge(s_blk, b + 2)
            if b >= 2:
                e.wait_ge(s_sc, 16 * (b - 1))
            z = PS[:, 4 + 2 * (b % 2):6 + 2 * (b % 2), :]
            e.activation(sbuf2[:, 2 * (b % 2):2 * (b % 2) + 2, :], z, ACT.Relu, scale=0.5).then_inc(s_zr, 1)

        @block.gpsimd
        def _(e):
            e.memset(R[:, LO:RN].bitcast(F32), 0.0).then_inc(s_init, 1)
            pool.run(e)
            for b in range(3):
                gather_y(e, b)
            y_lo(e, 0)
            for b in range(NB):
                if b + 1 < NB:
                    y_lo(e, b + 1)
                if b + 3 < NB:
                    gather_y(e, b + 3)
                scatter(e, b)
            e.wait_ge(s_sc, 16 * NB)

        @block.scalar
        def _(e):
            act.run(e)
            for b in range(NB):
                blk_hi(e, b)
                if b:
                    blk_out(e, b - 1)
            blk_out(e, NB - 1)

        RT = ytp
        OB = ring[:, 0:1280].rearrange("p (q b) -> p q b", b=NBP)
        OR = ring[:, 1280:1280 + 4096].rearrange("p (q r) -> p q r", r=128)

        @block.vector
        def _(e):
            n = [0]

            def link(ins):
                n[0] += 1
                ins.then_inc(s_v, 1)
                e.wait_ge(s_v, n[0])

            e.wait_ge(s_c, 32)
            link(e.tensor_copy(loraf[:, :], lorai[:, :]))
            link(e.scalar_tensor_tensor(out=idx_a[:, :], in0=loraf[:, :], scalar=128.0,
                                        in1=ci[:, 24:25].to_broadcast([128, 8]), op0=ALU.mult, op1=ALU.add))
            l3 = loraf[:, :].rearrange("p (b o) -> p b o", o=1)
            link(e.scalar_tensor_tensor(out=idx_b[:, :, :], in0=l3.to_broadcast([128, 8, NC]), scalar=352.0,
                                        in1=cB.rearrange("p (o c) -> p o c", o=1).to_broadcast([128, 8, NC]),
                                        op0=ALU.mult, op1=ALU.add))
            e.scalar_tensor_tensor(out=idx_d[:, :, :], in0=l3.to_broadcast([128, 8, 2]), scalar=32.0,
                                   in1=cD.rearrange("p (o c) -> p o c", o=1).to_broadcast([128, 8, 2]),
                                   op0=ALU.mult, op1=ALU.add).then_inc(s_idx, 3)
            dve.run(e)

            def bc(ap, shape):
                return ap.to_broadcast(shape)

            ids = mi[:, :, 0:2].rearrange("p t (s o) -> p s t o", o=1)
            oh = RT[:, 0:256].rearrange("p (s t e) -> p s t e", s=2, e=8)
            e.wait_ge(s_L, 18)
            link(e.tensor_tensor(oh, bc(io8.rearrange("p (a b e) -> p a b e", a=1, b=1), [128, 2, 16, 8]),
                                 bc(ids, [128, 2, 16, 8]), ALU.is_equal))
            e.tensor_tensor(msk[:, :, :], oh[:, 0], oh[:, 1], ALU.add).then_inc(s_m, 1)
            e.wait_ge(s_rk, 1)
            rk = PS[:, 0, 0:136].rearrange("p (t e) -> p t e", e=8)
            cmp1 = RT[:, 256:384].rearrange("p (e j) -> p e j", j=16)
            cmp2 = RT[:, 256:384].rearrange("p (e j) -> p e j", j=8)
            nb = RT[:, 384:392]
            cb, cbx = RT[:, 392:400], RT[:, 400:408]
            link(e.tensor_tensor(cmp1, bc(rk[:, 16, :].rearrange("p (e o) -> p e o", o=1), [128, 8, 16]),
                                 bc(thr.rearrange("p (o j) -> p o j", o=1), [128, 8, 16]), ALU.is_gt))
            link(e.tensor_reduce(nb, cmp1, AX.X, ALU.add))
            link(e.tensor_tensor(cmp2, bc(nb.rearrange("p (o j) -> p o j", o=1), [128, 16, 8]),
                                 tri.rearrange("p (e j) -> p e j", j=8), ALU.mult))
            link(e.tensor_reduce(RT[:, 392:408], cmp2, AX.X, ALU.add))
            R2 = RT[:, 408:536].rearrange("p (t e) -> p t e", e=8)
            link(e.scalar_tensor_tensor(out=R2, in0=bc(cbx.rearrange("p (o e) -> p o e", o=1), [128, 16, 8]),
                                        scalar=128.0, in1=rk[:, 0:16, :], op0=ALU.mult, op1=ALU.add))
            link(e.tensor_tensor(oh, oh, bc(R2.rearrange("p (o t) e -> p o t e", o=1), [128, 2, 16, 8]), ALU.mult))
            with nc.allow_low_precision(reason="whole numbers under 2^13"):
                link(e.tensor_reduce(posi[:, 0, :].rearrange("p (s t) -> p s t", s=2), oh, AX.X, ALU.add))
            e.tensor_scalar(posi[:, 1, :], posi[:, 0, :], 7, None, ALU.logical_shift_right)
            link(e.tensor_scalar(posi[:, 2, :], posi[:, 0, :], 127, None, ALU.bitwise_and))
            link(e.tensor_copy(rf[:, :], posi[:, 2, :]))
            link(e.tensor_tensor(OB, bc(io40.rearrange("p (o b) -> p o b", o=1), [128, 32, NBP]),
                                 bc(posi[:, 1, :].rearrange("p (q o) -> p q o", o=1), [128, 32, NBP]), ALU.is_equal))
            OB4 = OB.rearrange("p (s t) b -> p s t b", s=2)
            e.tensor_tensor(OB4, OB4, bc(tok1.rearrange("p (a t b) -> p a t b", a=1, b=1), [128, 2, 16, NBP]),
                            ALU.mult).then_inc(s_oh, 1)
            for q in range(32):
                m = e.tensor_scalar(OR[:, q, :], io128, rf[:, q:q + 1], None, ALU.is_equal)
                if q % 4 == 3:
                    m.then_inc(s_oh, 1)
            eb = RT[:, 672:712]
            cm2 = RT[:, 0:320].rearrange("p (b e) -> p b e", e=8)
            link(e.tensor_tensor(cm2, bc(io40.rearrange("p (b o) -> p b o", o=1), [128, NBP, 8]),
                                 bc(cb.rearrange("p (o e) -> p o e", o=1), [128, NBP, 8]), ALU.is_ge))
            link(e.tensor_reduce(eb, cm2, AX.X, ALU.add))
            link(e.tensor_scalar(eb, eb, 7.0, None, ALU.min))
            link(e.tensor_copy(meta[:, 80:80 + NBP], eb))
            link(e.tensor_scalar(meta[:, 0:NBP], meta[:, 80:80 + NBP], 1, None, ALU.bitwise_and))
            link(e.tensor_scalar(meta[:, NBP:2 * NBP], eb, 8.0, float(NP - 56), ALU.mult, ALU.add))
            link(e.tensor_scalar(meta[:, 120:128], cb, 1.0, None, ALU.add))
            e.tensor_tensor(oE[:, :], eb, ecol.to_broadcast([128, NBP]), ALU.is_equal).then_inc(s_meta, 1)
            e.wait_ge(s_rk, 2)
            pm1, isz = RT[:, 712:752], RT[:, 752:792]
            PM = PS[:, 1, 0:NBP]
            e.tensor_scalar(gidx[:, :], PM, -1.0, 0.0, ALU.add, ALU.max).then_inc(s_pm, 1)
            e.tensor_scalar(pm1, PM, -1.0, None, ALU.add)
            link(e.tensor_scalar(isz, PM, 0.0, dump, ALU.is_equal, ALU.mult))
            e.tensor_tensor(sidx[:, :], pm1, isz, ALU.add).then_inc(s_pm, 1)

            for ex in range(1, NE):
                if ex >= 2:
                    e.wait_ge(s_blk, e.value_load(meta[0:1, 118 + ex:119 + ex], min_val=1, max_val=NB + 1))
                for k in range(8):
                    if (ex, k) in EARLY:
                        continue
                    i = at[("e", ex, k)]
                    arrived(e, i)
                    link(e.tensor_copy(s_w_t(ex, k, 0), raw[:, i % RW, :]))
                    e.tensor_tensor(s_w_t(ex, k, 1), raw[:, i % RW, :], s_w_t(ex, k, 0), ALU.subtract).then_inc(s_lo, 1)


        @block.tensor
        def _(e):
            def mm3(out_, hi, lo, whi, wlo, start, stop=False):
                e.matmul(out_, hi, whi, start=start, stop=False)
                e.matmul(out_, hi, wlo, start=False, stop=False)
                return e.matmul(out_, lo, whi, start=False, stop=stop)

            def lora_in(g):
                e.wait_ge(s_ll, 2 * g + 2)
                for b in range(2):
                    for k in range(8):
                        for part in range(2):
                            m = e.matmul(PS[:, 2, b * 256:(b + 1) * 256], a_t(b)[:, k * 64:k * 64 + 128],
                                         x_t(part, k)[:, b * 256:(b + 1) * 256], start=(k == 0 and part == 0),
                                         stop=(k == 7 and part == 1))
                m.then_inc(s_t, 1)

            def lora_out(g, c, bank, q, last):
                n = g * 26 + c
                e.wait_ge(s_bl, n + 1)
                e.wait_ge(s_tl, 3 * g + 2)
                for b in range(2):
                    o = b * 256 + q * 128
                    m = e.matmul(PS[:, bank, b * 256:(b + 1) * 256], b_t(n % 2)[:, o:o + 128],
                                 TT[:, q, b * 256:(b + 1) * 256], start=False, stop=last and b == 1)
                return m

            def first(g, c, q):
                n = g * NU + 2 * c + q
                bank = 2 * (c % 2) + q
                m0 = g * NC + c
                e.wait_ge(s_lo, at[("w", g, 2 * c + q)] + 1)
                if m0 >= 2:
                    if q == 0:
                        e.wait_ge(s_silu, m0 - 1)
                    else:
                        e.wait_ge(s_a, m0 - 1)
                if c % 2 == 0 and g:
                    e.wait_ge(s_u21, g)
                if c == 0 and g:
                    e.wait_ge(s_ya, 4 * g - 2)
                    e.wait_ge(s_yd, 4 * g - 2)
                w = [ring_t(n, 0), ring_t(n, 1)]
                for k in range(8):
                    sl = slice(k * 128, (k + 1) * 128)
                    if c == 0 and q == 0 and k % 2 == 0:
                        e.wait_ge(s_lo, at[("x", g, k // 2)] + 1)
                    e.matmul(PS[:, bank, :], w[0][:, sl], x_t(0, k), start=(k == 0), stop=False)
                    e.matmul(PS[:, bank, :], w[0][:, sl], x_t(1, k), start=False, stop=False)
                    e.matmul(PS[:, bank, :], w[1][:, sl], x_t(0, k), start=False, stop=False)
                if c == NC - 1:
                    lora_out(g, c, bank, 0, False)
                    lora_out(g, c, bank, 1, True).then_inc(s_pe, 1)
                elif c == 0:
                    if q == 0:
                        lora_in(g)
                    else:
                        lora_out(g, 0, 0, 0, True).then_inc(s_pe, 1)
                        lora_out(g, 0, 1, 1, True).then_inc(s_pe, 1)
                else:
                    lora_out(g, c, bank, q, True).then_inc(s_pe, 1)

            def lora_down_in(g, c):
                e.wait_ge(s_act, g * NC + c + 1)
                if c == 0 and g:
                    e.wait_ge(s_ya, 4 * g)
                for part in range(2 if c < NC - 1 else 1):
                    for b in range(2):
                        m = e.matmul(PS[:, 4, b * 256:(b + 1) * 256], a_t(b)[:, (16 + c) * 32:(16 + c) * 32 + 128],
                                     act_t(c, part)[:, b * 256:(b + 1) * 256],
                                     start=(c == 0 and part == 0 and b == 0), stop=(c == NC - 1),
                                     skip_group_check=True)
                if c == NC - 1:
                    m.then_inc(s_t, 1)

            def down(g, h, j):
                n = unit_down(g, h, j)
                e.wait_ge(s_lo, at[("w", g, n - g * NU)] + 1)
                e.wait_ge(s_act, g * NC + 2 * j + 2 if h == 0 else g * NC + NC)
                if j == 0 and h == 0:
                    e.wait_ge(s_a, g * NC + NC - 1)
                    e.wait_ge(s_u21, g + 1)
                if j == 0 and h == 1:
                    e.wait_ge(s_tl, 3 * g + 3)
                    if g:
                        e.wait_ge(s_lm, 64 * g)
                w = [ring_t(n, 0), ring_t(n, 1)]

                def part(tt, cc):
                    c = 2 * j + cc
                    o = PS[:, 4 * h + tt, :]
                    ts = slice(tt * 128, (tt + 1) * 128)
                    whi, wlo = (x[:, cc * 512:(cc + 1) * 512] for x in w)
                    if c < NC - 1:
                        return mm3(o, act_t(c, 0)[:, ts], act_t(c, 1)[:, ts], whi, wlo, start=(c == 0))
                    e.matmul(o, act_t(c, 0)[:, ts], whi, start=False, stop=False)
                    return e.matmul(o, act_t(c, 0)[:, ts], wlo, start=False, stop=False)

                if j < 10:
                    for cc in range(2):
                        for tt in range(4):
                            m = part(tt, cc)
                    m.then_inc(s_pe, 1)
                    return
                e.wait_ge(s_tl, 3 * g + 3)
                e.wait_ge(s_bl, g * 26 + NC + 2 * h + 2)
                for tt in range(4):
                    if g == NG - 1 and h == 1:
                        if tt >= 2:
                            logit_turn(LT_AT[10 + tt, 1])
                        if tt >= 3:
                            logit_sum(LT_AT[9 + tt, 1])
                    part(tt, 0)
                    part(tt, 1)
                    nb_ = g * 26 + NC + 2 * h + tt // 2
                    e.matmul(PS[:, 4 * h + tt, :], TT[:, 2, tt * 128:(tt + 1) * 128], b_t(nb_ % 2),
                             start=False, stop=True).then_inc(s_z if tt < 3 else s_pe, 1)

            def logit_turn(m):
                q, h, slot = LT[m]
                g, tt = NG - 1, q % 4
                if m == 0:
                    e.wait_ge(s_cb, 80)
                if m >= 2:
                    e.wait_ge(s_lc, m - 1)
                e.wait_ge(s_yd if tt % 2 else s_ya, 4 * g + 2 * h + tt // 2 + 1)
                for k in range(4):
                    i = e.transpose(PS[:, slot, k * 128:(k + 1) * 128],
                                    ybuf[:, tt, h * 512 + k * 128:h * 512 + (k + 1) * 128], ident[:, :])
                i.then_inc(s_lt, 1)

            def logit_sum(m):
                q, h, slot = LT[m]
                e.wait_ge(s_lc, m + 1)
                col = 8 * (q % 4)
                for k in range(4):
                    i = e.matmul(PS[:, 2 + (q - 12) // 2, col:col + 8],
                                 ytp[:, slot * 512 + k * 128:slot * 512 + (k + 1) * 128], wg_s[:, 4 * h + k, :],
                                 start=(k == 0 and h == 0 and q % 2 == 0), stop=(k == 3 and h == 1),
                                 skip_group_check=True)
                i.then_inc(s_lg, 1)

            for g in range(NG):
                for c in range(NC):
                    first(g, c, 0)
                    if c:
                        lora_down_in(g, c - 1)
                    if c < NC - 1:
                        first(g, c, 1)
                for h in range(2):
                    for j in range(11):
                        down(g, h, j)
                        if h == 0 and j == 0:
                            lora_down_in(g, NC - 1)
                        if g == NG - 1 and h == 1:
                            if 1 <= j <= 4:
                                logit_turn(LT_AT[11 + j, 0])
                            if 2 <= j <= 5:
                                logit_sum(LT_AT[10 + j, 0])
            last = [LT_AT[12 + t, 1] for t in range(4)]
            logit_turn(last[2])
            logit_sum(last[1])
            logit_turn(last[3])
            logit_sum(last[2])
            logit_sum(last[3])

            def keep_warm(n):
                for _ in range(n):
                    e.matmul(PS[:, 5, 0:256], ut[:, 0:128], ut[:, :], start=True, stop=True)

            keep_warm(15)
            e.wait_ge(s_m, 1)
            rk = PS[:, 0, 0:136].rearrange("p (t e) -> p t e", e=8)
            for t in range(16):
                n_ = 16 - t
                e.matmul(rk[:, t + 1:17, :], ut[:, 128:256],
                         msk[:, t:t + 1, :].to_broadcast([128, n_, 8]), start=(t == 0), stop=False,
                         skip_group_check=True)
            e.matmul(rk[:, 0:16, :], ut[:, 0:128], msk[:, :, :], start=False, stop=True,
                     skip_group_check=True).then_inc(s_rk, 1)
            keep_warm(30)
            for q in range(32):
                if q % 4 == 0:
                    e.wait_ge(s_oh, q // 4 + 2)
                m = e.matmul(PS[:, 1, 0:NBP], OR[:, q, :], OB[:, q, :], start=(q == 0), stop=(q == 31))
            m.then_inc(s_rk, 1)

            def turn(b):
                e.wait_ge(s_gd[b % 3], 16 * (b // 3 + 1))
                if b >= 2:
                    e.wait_ge(s_tc, b - 1)
                for k in range(8):
                    m = e.transpose(PS[:, 2 * (b % 2) + k // 4, (k % 4) * 128:(k % 4 + 1) * 128],
                                    ybuf[:, b % 3, k * 128:(k + 1) * 128], ident[:, :])
                    if b == 0 and k == 0:
                        m.then_inc(s_blk, 1)
                m.then_inc(s_tp, 1)

            e.wait_ge(s_meta, 1)
            used = e.value_load(meta[0:1, 127:128], min_val=1, max_val=NB + 1)
            keep_warm(20)
            turn(0)
            keep_warm(15)
            e.wait_ge(s_bias, 2)
            for b in range(NB):
                side = e.value_load(meta[0:1, b:b + 1], min_val=0, max_val=1)
                ready = e.value_load(meta[0:1, NBP + b:NBP + b + 1], min_val=NP - 56, max_val=NP)
                off = e.snap(side * 16384)
                e.wait_ge(s_tc, b + 1)
                e.wait_ge(s_tlo, b + 1)
                e.wait_ge(s_lo, ready)
                if b >= 2:
                    e.wait_ge(s_zr, b - 1)

                def products(ks):
                    for k in ks:
                        kk = slice(k * 128, (k + 1) * 128)
                        hi, lo = ring_t(b % 2, 0)[:, kk], ring_t(b % 2, 1)[:, kk]
                        for n in range(2):
                            o = PS[:, 4 + 2 * (b % 2) + n, :]
                            w = [R[:, bass.ds(off + (k * 2048 + p * 1024 + n * 512), 512)] for p in range(2)]
                            mm3(o, hi, lo, w[0], w[1], start=(k == 0))

                def add_bias(start):
                    for n in range(2):
                        m = e.matmul(PS[:, 4 + 2 * (b % 2) + n, :], oE[:, b:b + 1].to_broadcast([128, 128]),
                                     bias[:, n * 512:(n + 1) * 512], start=start, stop=True)
                    m.then_inc(s_blk, 1)

                if b < 32:
                    products(range(4))
                    turn(b + 1)
                    products(range(4, 8))
                    add_bias(False)
                else:
                    if b + 1 < NB:
                        turn(b + 1)
                    with e.If(used > b + 1):
                        products(range(8))
                        add_bias(False)
                    with e.Else():
                        add_bias(True)


def tables():
    import numpy as np

    p = np.arange(128)
    cf = np.zeros((128, 352), np.float32)
    cf[:, 0:16] = 128 * np.arange(16) + p[:, None] + 1
    cf[:, 16:24] = np.arange(8)
    cf[:, 24:64] = np.arange(40)
    cf[:, 64:80] = 128 * np.arange(16)
    e = np.arange(8)
    cf[:, 80:144] = (e[None, :] <= e[:, None]).reshape(-1)
    cf[:, 144:208] = (e[None, :] < e[:, None]).reshape(-1)
    cf[:, 208:336] = np.arange(128)
    cf[:, 336] = 2049 + p
    cf[:, 337] = np.where(p < 8, p, np.where((p >= 32) & (p < 40), p - 32, -1))
    ci = np.zeros((128, 32), np.float32)
    ci[:, 0:22] = ((p % 16) * 22)[:, None] + np.arange(22)
    ci[:, 22:24] = ((p % 16) * 2)[:, None] + np.arange(2)
    ci[:, 24] = p
    ut = np.concatenate([(p[:, None] < p[None, :]), np.ones((128, 128), bool)], 1)
    return cf, ci, np.eye(128, dtype=np.float32), ut


def kernel(**inputs):
    import ml_dtypes
    import numpy as np
    import concourse.bacc as bacc
    from concourse import mybir as mb
    from concourse.bass_utils import run_bass_kernel_spmd as run

    A = {k: np.asarray(v) for k, v in inputs.items()}
    x = A["x"].reshape(T, H)
    xp = x.reshape(4, 512, 4, 2, 128).transpose(0, 2, 4, 3, 1).reshape(16, 128, 1024)

    def first(w):
        n = w.shape[0] // 128
        return w.reshape(n, 128, 8, 128).transpose(0, 3, 2, 1).reshape(n, 128, 1024)

    wg, wu, wd = A["L0_cond_W_gate"], A["L0_cond_W_up"], A["L0_cond_W_down"]
    g21, u21 = first(wg[:2688]), first(wu[:2688])
    both = first(np.concatenate([wg[2688:], wu[2688:]], 0))
    wdt = wd.T
    wdt = np.concatenate([wdt, wdt[2688:]], 0)
    dn = wdt.reshape(11, 2, 128, 2, 512).transpose(3, 0, 2, 1, 4).reshape(22, 128, 1024)
    wp = np.concatenate([np.stack([g21, u21], 1).reshape(42, 128, 1024), both, dn], 0)

    ag, au, ad = (A["L0_cond_A_" + n][0] for n in ("gate", "up", "down"))
    agu = np.stack([ag, au], 1).reshape(16, 2, 16, 8, 128).transpose(0, 4, 3, 1, 2).reshape(16, 128, 256)
    adt = np.concatenate([ad, ad[:, :, 2688:]], 2)
    adt = adt.reshape(16, 16, 22, 128).transpose(0, 3, 2, 1).reshape(16, 128, 352)
    at_ = np.concatenate([agu, adt], 2).reshape(2048, 608)

    bgt, but, bdt = (A["L0_cond_B_" + n][0].transpose(0, 2, 1) for n in ("gate", "up", "down"))
    z = np.zeros((16, 16, 64), np.float32)
    bgt = np.concatenate([bgt, z], 2).reshape(16, 16, 22, 1, 128)
    but = np.concatenate([but[:, :, :2688], z, but[:, :, 2688:]], 2).reshape(16, 16, 22, 1, 128)
    bgu = np.concatenate([bgt, but], 3).reshape(16 * 16 * 22, 256)
    bdn = bdt.reshape(16 * 16 * 2, 512)

    wgt = A["L0_ffn_W_gate"].reshape(8, 128, 8).transpose(1, 0, 2)
    wgb = A["L0_ffn_W_gate"].reshape(2, 512, 8).transpose(0, 2, 1).reshape(16, 512)
    we = A["L0_ffn_W_e"].reshape(8, 8, 128, 1024)
    cf, ci, ident, ut = tables()
    arrays = {
        "xp": xp, "xn": x, "wp": wp, "agu": at_, "bgu": bgu, "bdn": bdn,
        "itok": A["itok_B_2_6"], "wgt": wgt, "wgb": wgb, "bg": A["L0_ffn_b_gate"], "we": we, "be": A["L0_ffn_b_e"],
        "cst_f": cf, "cst_i": ci, "ident": ident, "ut": ut.astype(ml_dtypes.bfloat16),
    }
    arrays = {k: np.ascontiguousarray(v) for k, v in arrays.items()}
    nc = bacc.Bacc("TRN2", target_bir_lowering=False, num_devices=1, dynamic_dma_scratch_size=4096)
    args = [nc.dram_tensor(f"in_{k}", v.shape, mb.dt.from_np(v.dtype), kind="ExternalInput").ap()
            for k, v in arrays.items()]
    out = nc.dram_tensor("out_0", (T + 128, H), mb.dt.float32, kind="ExternalOutput").ap()
    build(nc, *args, out)
    r = run(nc, [{f"in_{k}": v for k, v in arrays.items()}], core_ids=[0])
    return r.results[0]["out_0"][:T].reshape(8, 256, 1024)
```

```python
from contextlib import ExitStack

import concourse.bass as bass
from concourse import mybir

F32 = mybir.dt.float32
F32R = mybir.dt.float32r
BF16 = mybir.dt.bfloat16
I32 = mybir.dt.int32
U32 = mybir.dt.uint32
ALU = mybir.AluOpType
ACT = mybir.ActivationFunctionType
AX = mybir.AxisListType

T = 2048
H = 1024
F = 2752
NG = 4
NC = 22
NU = 65
S2 = 43
NE = 8
ET = 12
NB = 41
RW = 3
XAT = [S2 + 4, S2 + 7, S2 + 10, S2 + 13]


EARLY = {(0, 0): S2 + 3, (0, 1): S2 + 5, (0, 2): S2 + 7, (0, 3): S2 + 9, (0, 4): S2 + 15, (0, 5): S2 + 16,
         (0, 6): S2 + 17, (0, 7): S2 + 18, (1, 0): S2 + 19, (1, 1): S2 + 20, (1, 2): S2 + 21}


class Jobs:

    def __init__(self):
        self.jobs = []

    def add(self, key, fn, *args):
        self.jobs.append((key, len(self.jobs), fn, args))

    def run(self, eng):
        for _, _, fn, args in sorted(self.jobs, key=lambda j: j[:2]):
            fn(eng, *args)


def unit_gate(g, c):
    return g * NU + 2 * c


def unit_up(g, c):
    return g * NU + (2 * c + 1 if c < NC - 1 else 2 * c)


def unit_down(g, h, j):
    return g * NU + S2 + 11 * h + j


def piece_list():
    out = [("w", 0, 0)] + [("x", 0, i) for i in range(4)]
    for g in range(NG):
        for n in range(NU):
            if g + 1 < NG and n in XAT:
                out.append(("x", g + 1, XAT.index(n)))
            if g == NG - 1:
                out += [("e", e, k) for e, k in EARLY if EARLY[e, k] == n]
            if (g, n) != (0, 0):
                out.append(("w", g, n))
    for e in range(NE):
        for k in range(8):
            if (e, k) not in EARLY:
                out.append(("e", e, k))
    return out


def build(nc, xp, xn, wp, agu, bgu, bdn, itok, wgt, wgb, bg, we, be, cst_f, cst_i, ident_d, ut_d, out):
    pieces = piece_list()
    at = {p: i for i, p in enumerate(pieces)}
    LT = [(12 + t, 1, t % 2) for t in range(4)]
    LT_AT = {(q, h): m for m, (q, h, _) in enumerate(LT)}
    NP = len(pieces)

    ctx = ExitStack()
    with ctx:
        def sb(name, shape, dt):
            return ctx.enter_context(nc.sbuf_tensor(name, shape, dt))

        def sem(name):
            return ctx.enter_context(nc.semaphore(name))

        XO, AO = 0, 8192
        BO = AO + 21 * 1024 + 512
        LO = BO + 2 * 512
        LA = 38 * 32 + 96
        RN = LO + 2 * LA
        R = sb("R", [128, RN], F32R)
        ring = sb("ring", [128, RW * 2048], F32R)
        TT = sb("TT", [96, 3, 512], F32R)
        raw = sb("raw", [128, RW, 1024], F32)
        AB = sb("AB", [128, 2240], F32)
        braw = AB[0:96, 0:1024].rearrange("p (a n) -> p a n", a=2)
        araw = AB[:, 1024:2240].rearrange("p (a n) -> p a n", a=2)
        ybuf = sb("ybuf", [128, 4, 1024], F32)
        sbuf2 = sb("sbuf2", [128, 4, 512], F32)
        ytp = sb("ytp", [128, 1024], F32)
        ident = sb("ident", [128, 128], F32)
        ut = sb("ut", [128, 256], BF16)
        cf = sb("cf", [128, 352], F32)
        ci = sb("ci", [128, 32], F32)
        wg_s = sb("wg_s", [128, 8, 8], F32)
        bg_s = sb("bg_s", [128, 8], F32)
        Lp = sb("Lp", [128, 2, 4, 8], F32)
        Lg = sb("Lg", [128, 16, 8], F32)
        mx = sb("mx", [128, 16, 8], F32)
        mi = sb("mi", [128, 16, 8], U32)
        lorai = sb("lorai", [128, 8], I32)
        loraf = sb("loraf", [128, 8], F32)
        idx_a = sb("idx_a", [128, 8], U32)
        idx_b = sb("idx_b", [128, 8, NC], U32)
        idx_d = sb("idx_d", [128, 8, 2], U32)
        gidx = sb("gidx", [128, NB], U32)
        sidx = sb("sidx", [128, NB], U32)
        meta = sb("meta", [128, 136], I32)
        msk = sb("msk", [128, 16, 8], BF16)
        oh = sb("oh", [128, 2, 16, 8], BF16)
        posi = sb("posi", [128, 3, 32], U32)
        PS = ctx.enter_context(nc.psum_tensor("PS", [128, 8, 512], F32))

        def x_t(part, k):
            return R[:, XO + part * 4096 + k * 512: XO + part * 4096 + (k + 1) * 512]

        def act_t(c, part):
            o = AO + c * 1024 + part * 512
            return R[:, o:o + 512]

        def b_t(slot):
            return R[0:96, BO + slot * 512: BO + (slot + 1) * 512]

        def a_t(b):
            return R[:, LO + b * LA: LO + (b + 1) * LA]

        def ring_t(n, part):
            o = (n % RW) * 2048 + part * 1024
            return ring[:, o:o + 1024]

        def slot_of(i):
            return i if i in (RW, RW + 1) else i % RW

        def raw_t(i):
            return ybuf[:, i - RW, :] if i in (RW, RW + 1) else raw[:, i % RW, :]

        def s_w_t(e, k, part):
            o = (e % 2) * 16384 + k * 2048 + part * 1024
            return R[:, o:o + 1024]

        s_x00 = sem("s_x00")
        s_w0, s_w0h, s_w0l = sem("s_w0"), sem("s_w0h"), sem("s_w0l")
        s_c = sem("s_c")
        s_cb = sem("s_cb")
        s_init = sem("s_init")
        s_idx = sem("s_idx")
        s_raw = [sem(f"s_raw{i}") for i in range(RW + 2)]
        s_hi, s_lo = sem("s_hi"), sem("s_lo")
        s_pe = sem("s_pe")
        s_silu, s_a, s_ah = sem("s_silu"), sem("s_a"), sem("s_ah")
        s_act, s_u21 = sem("s_act"), sem("s_u21")
        s_braw = [sem("s_braw0"), sem("s_braw1")]
        s_bh, s_bl = sem("s_bh"), sem("s_bl")
        s_ar, s_lh, s_ll = sem("s_ar"), sem("s_lh"), sem("s_ll")
        s_t, s_th, s_tl = sem("s_t"), sem("s_th"), sem("s_tl")
        s_z = sem("s_z")
        s_ya, s_yd = sem("s_ya"), sem("s_yd")
        s_yst, s_y0, s_y1 = sem("s_yst"), sem("s_y0"), sem("s_y1")
        s_lt, s_lc, s_lg, s_L = sem("s_lt"), sem("s_lc"), sem("s_lg"), sem("s_L")
        s_wb = [sem("s_wb0"), sem("s_wb1")]
        s_lm, s_lb = sem("s_lm"), sem("s_lb")
        s_x0 = sem("s_x0")
        s_v = sem("s_v")
        s_m = sem("s_m")
        s_rk = sem("s_rk")
        s_ep, s_ee = sem("s_ep"), sem("s_ee")
        s_ge = [sem("s_ge0"), sem("s_ge1")]
        s_oe, s_pos, s_ob = sem("s_oe"), sem("s_pos"), sem("s_ob")
        s_f, s_f0, s_f1 = sem("s_f"), sem("s_f0"), sem("s_f1")
        s_oh, s_pm, s_meta = sem("s_oh"), sem("s_pm"), sem("s_meta")
        s_bias, s_zc, s_ba = sem("s_bias"), sem("s_zc"), sem("s_ba")
        s_gd = [sem(f"s_gd{i}") for i in range(3)]
        s_tp, s_tc, s_tlo = sem("s_tp"), sem("s_tc"), sem("s_tlo")
        s_blk, s_zr, s_sc = sem("s_blk"), sem("s_zr"), sem("s_sc")

        y_d = nc.dram_tensor("y_scratch", (T, H), F32).ap()

        tok1 = cf[:, 0:16]
        io8 = cf[:, 16:24]
        thr = cf[:, 64:80]
        tri = cf[:, 80:208]
        io128 = cf[:, 208:336]
        io_b = io128[:, 0:NB]
        dump = cf[:, 336:337]
        cB = ci[:, 0:22]
        cD = ci[:, 22:24]

        block = ctx.enter_context(nc.Block())

        def logit_unit(o):
            return 2 * (o // 3)

        @block.sync
        def _(sp):
            def load(i):
                kind, a, b = pieces[i]
                if i > RW + 1:
                    sp.wait_ge(s_lo, i - RW + 1)
                if kind == "x":
                    src = xp[a * 4 + b]
                elif kind == "w":
                    src = wp[b]
                else:
                    src = we[a, b]
                sp.dma_start(raw_t(i), src).then_inc(s_raw[slot_of(i)], 16)

            def wb_before(n):
                g, s = divmod(n, 16)
                if g == NG - 1:
                    return "w", g, 50 + s if s < 2 else 56 + s
                if s < 2:
                    return "w", g, 55 + s
                return "w", g + 1, logit_unit(4 * (s - 2) + 3) + 7

            def load_wb(n):
                if n >= 2:
                    sp.wait_ge(s_lm, 4 * (n - 1))
                sp.dma_start(ytp[:, (n % 2) * 512:(n % 2) * 512 + 512],
                             wgb[n % 16].partition_broadcast(128)).then_inc(s_wb[n % 2], 16)

            def load_bias(ex):
                if ex < 2:
                    sp.wait_ge(s_ee, 3)
                    sp.wait_ge(s_ll, 2 * NG)
                    sp.wait_ge(s_bl, 26 * NG)
                else:
                    sp.wait_ge(s_meta, 1)
                    sp.wait_ge(s_ba, sp.value_load(meta[0:1, 3 * NB + ex - 2:3 * NB + ex - 1], min_val=1, max_val=NB + 1))
                if ex:
                    sp.wait_ge(s_bias, 16 * ex)
                sp.dma_start(AB[:, (ex % 2) * 1024:(ex % 2) * 1024 + 1024],
                             be[ex].partition_broadcast(128)).then_inc(s_bias, 16)

            sp.dma_start(raw[:, 0, 0:512], wp[0][:, 0:512]).then_inc(s_w0, 16)
            sp.dma_start(raw[:, 1, 0:512], xp[0][:, 0:512]).then_inc(s_x00, 16)
            sp.dma_start(raw[:, 1, 512:1024], xp[0][:, 512:1024]).then_inc(s_raw[1], 16)
            sp.dma_start(raw[:, 0, 512:1024], wp[0][:, 512:1024]).then_inc(s_raw[0], 16)
            sp.dma_start(lorai[:, :], itok.partition_broadcast(128)).then_inc(s_c, 16)
            sp.dma_start(ci[:, :], cst_i).then_inc(s_c, 16)
            load(2)
            load(3)
            load(4)
            for dst, src in ((ident[:, :], ident_d), (ut[:, :], ut_d), (cf[:, :], cst_f), (wg_s[:, :, :], wgt),
                             (bg_s[:, :], bg.partition_broadcast(128))):
                sp.dma_start(dst, src).then_inc(s_cb, 16)
            wb = {}
            for n in range(56):
                wb.setdefault(at[wb_before(n)], []).append(n)
            for i in range(RW + 2, len(pieces)):
                for n in wb.get(i, ()):
                    load_wb(n)
                if i in (at["e", 1, 0], at["e", 1, 2]):
                    load_bias(pieces[i][2] // 2)
                if pieces[i][0] == "e" and pieces[i][1] >= 2 and pieces[i][2] == 3:
                    load_bias(pieces[i][1])
                load(i)

        pool = Jobs()

        def ioa(ap):
            return bass.IndirectOffsetOnAxis(ap=ap, axis=0)

        def gather_a(e, g):
            if g == 0:
                e.wait_ge(s_idx, 3)
            else:
                e.wait_ge(s_ll, 2 * g)
            for b in range(2):
                e.indirect_dma_start(out=araw[:, b, :], out_offset=None, in_=agu,
                                     in_offset=ioa(idx_a[:, 2 * g + b:2 * g + b + 1])).then_inc(s_ar, 16)

        def gather_b(e, g, i):
            n = g * 26 + i
            if n >= 2:
                e.wait_ge(s_bl, n - 1)
            if i < NC:
                for b in range(2):
                    e.indirect_dma_start(out=braw[:, n % 2, b * 256:(b + 1) * 256], out_offset=None, in_=bgu,
                                         in_offset=ioa(idx_b[0:96, 2 * g + b, i:i + 1])).then_inc(s_braw[n % 2], 16)
            else:
                h, b = divmod(i - NC, 2)
                e.indirect_dma_start(out=braw[:, n % 2, :], out_offset=None, in_=bdn,
                                     in_offset=ioa(idx_d[0:96, 2 * g + b, h:h + 1])).then_inc(s_braw[n % 2], 16)

        def braw_value(n):
            return 16 * sum(2 if m % 26 < NC else 1 for m in range(n % 2, n + 1, 2))

        def b_use(g, i):
            if i < NC:
                return unit_up(g, i)
            return unit_down(g, (i - NC) // 2, 10)

        def store_y(e, g, h, t0, t1):
            e.wait_ge(s_ya, 4 * g + 2 * h + (t1 + 1) // 2)
            e.wait_ge(s_yd, 4 * g + 2 * h + t1 // 2)
            cols = slice(h * 512, (h + 1) * 512)
            e.dma_start(y_d[g * 512 + t0 * 128:g * 512 + t1 * 128, cols].rearrange("(t p) n -> p t n", p=128),
                        ybuf[:, t0:t1, cols]).then_inc(s_yst if t1 - t0 == 4 else s_y1 if t0 else s_y0, 16)

        def copy_x(e, g):
            e.dma_start(out[g * 512:(g + 1) * 512, :], xn[g * 512:(g + 1) * 512, :]).then_inc(s_x0, 16)
            if g == 0:
                e.dma_start(out[T:T + 128, :], xn[0:128, :]).then_inc(s_x0, 16)

        for g in range(NG):
            pool.add(g * NU - 30, gather_a, g)
            for i in range(26):
                n = g * 26 + i
                p2 = n - 2
                pool.add(b_use(p2 // 26, p2 % 26) - 6 if n >= 2 else -20, gather_b, g, i)
            pool.add(g * NU + 10, lambda e, g=g: (e.wait_ge(s_pe, g * NU + 6), copy_x(e, g)))
            pool.add(g * NU + NU - 11, store_y, g, 0, 0, 4)
            if g < NG - 1:
                pool.add(g * NU + NU - 0.5, store_y, g, 1, 0, 4)
            else:
                for t in range(4):
                    pool.add(g * NU + NU - 0.5, store_y, g, 1, t, t + 1)

        flat = ybuf[:, :, :].rearrange("p a n -> p (a n)")
        RT = flat[:, 0:672]
        OR = flat[:, 672:2720].bitcast(BF16).rearrange("p (q r) -> p q r", r=128)
        OB = flat[:, 2720:2720 + 32 * NB].bitcast(BF16).rearrange("p (s t a b) -> p s t a b", s=2, t=16, a=2)

        def block_hots(e):
            for s in range(2):
                e.wait_ge(s_pos, s + 1)
                e.tensor_tensor(OB[:, s, :, 1], OB[:, s, :, 0], tok1[:, 0:1].rearrange("p (t b) -> p t b", b=1)
                                .to_broadcast([128, 16, NB]), ALU.mult).then_inc(s_ob, 1)
                e.wait_ge(s_ob, 2 * s + 1)
                e.tensor_tensor(OB[:, s, :, 0], OB[:, s, :, 0], thr.rearrange("p (t b) -> p t b", b=1)
                                .to_broadcast([128, 16, NB]), ALU.mult).then_inc(s_ob, 1)

        def gather_y(e, b):
            if b < 2:
                e.wait_ge(s_ee, 3)
                e.wait_ge(s_act, NG * NC)
                e.wait_ge(s_yst, 16 * 2 * (NG - 1))
                e.indirect_dma_start(out=early_y(b), out_offset=None, in_=y_d[0:128 * ET, :],
                                     in_offset=ioa(gidx[:, b:b + 1])).then_inc(s_ge[b], 16)
                return
            if b in (2, 3):
                e.wait_ge(s_pm, b - 1)
            if b >= 5:
                e.wait_ge(s_tp, b - 2)
            e.indirect_dma_start(out=ybuf[:, b % 3, :], out_offset=None, in_=y_d,
                                 in_offset=ioa(gidx[:, b:b + 1])).then_inc(s_gd[b % 3], 16)

        def early_y(b):
            return sbuf2[:, 2 * b:2 * b + 2, :].rearrange("p a n -> p (a n)")

        pool.add(unit_down(NG - 1, 0, 5), lambda e: (gather_y(e, 0), gather_y(e, 1)))

        def y_lo(e, b):
            e.wait_ge(s_tc, b + 1)
            e.tensor_tensor(ring_t(b % 2, 1), ytp[:, :], ring_t(b % 2, 0), ALU.subtract).then_inc(s_tlo, 1)

        def add_bias(e, b):
            side, ready = 0, 16
            if b >= 2:
                side = e.value_load(meta[0:1, b:b + 1], min_val=0, max_val=1)
                ready = e.value_load(meta[0:1, 2 * NB + b:2 * NB + b + 1], min_val=16, max_val=16 * NE)
            e.wait_ge(s_zc, b + 1)
            e.wait_ge(s_bias, ready)
            z = sbuf2[:, 2 * (b % 2):2 * (b % 2) + 2, :].rearrange("p a n -> p (a n)")
            e.tensor_tensor(z, z, AB[:, bass.ds(e.snap(side * 1024), 1024)] if b >= 2 else AB[:, 0:1024], ALU.add).then_inc(s_ba, 1)

        def scatter(e, b):
            e.wait_ge(s_zr, b + 1)
            if b:
                e.wait_ge(s_sc, 16 * b)
            else:
                e.wait_ge(s_x0, 16 * (NG + 1))
            e.indirect_dma_start(out=out, out_offset=ioa(sidx[:, b:b + 1]),
                                 in_=sbuf2[:, 2 * (b % 2):2 * (b % 2) + 2, :].rearrange("p a n -> p (a n)"),
                                 in_offset=None, compute_op=ALU.add).then_inc(s_sc, 16)

        act = Jobs()
        dve = Jobs()

        def arrived(e, i):
            e.wait_ge(s_raw[slot_of(i)], 16 * sum(slot_of(j) == slot_of(i) for j in range(i + 1)))

        def piece_dst(i, part):
            kind, a, b = pieces[i]
            if kind == "x":
                o = XO + part * 4096 + b * 1024
                return R[:, o:o + 1024]
            if kind == "e":
                return s_w_t(a, b, part)
            return ring_t(a * NU + b, part)

        def early_after(e, k):
            j = 8 * e + k - 4
            return unit_down(NG - 1, 1, j) if j >= 0 else unit_up(NG - 1, NC - 1)

        def split_hi(e, i):
            kind, a, b = pieces[i]
            if i == 0:
                e.wait_ge(s_w0, 16)
                e.activation(ring_t(0, 0)[:, 0:512], raw[:, 0, 0:512], ACT.Copy).then_inc(s_w0h, 1)
                return
            if i == 1:
                e.wait_ge(s_x00, 16)
                e.activation(x_t(0, 0), raw[:, 1, 0:512], ACT.Copy).then_inc(s_w0h, 1)
                arrived(e, 1)
                e.activation(x_t(0, 1), raw[:, 1, 512:1024], ACT.Copy).then_inc(s_w0h, 1)
                arrived(e, 0)
                e.activation(ring_t(0, 0)[:, 512:1024], raw[:, 0, 512:1024], ACT.Copy).then_inc(s_hi, 2)
                return
            arrived(e, i)
            if kind == "w":
                n = a * NU + b
                if n >= RW:
                    e.wait_ge(s_pe, n - RW + 1)
            elif kind == "e":
                e.wait_ge(s_pe, early_after(a, b) + 1)
            elif a > 0:
                e.wait_ge(s_pe, (a - 1) * NU + S2)
            e.activation(piece_dst(i, 0), raw_t(i), ACT.Copy).then_inc(s_hi, 1)

        def split_lo(e, i):
            if i == 0:
                e.wait_ge(s_w0h, 1)
                e.tensor_tensor(ring_t(0, 1)[:, 0:512], raw[:, 0, 0:512], ring_t(0, 0)[:, 0:512],
                                ALU.subtract).then_inc(s_w0l, 1)
                return
            if i == 1:
                for k in range(2):
                    e.wait_ge(s_w0h, 2 + k)
                    e.tensor_tensor(x_t(1, k), raw[:, 1, k * 512:k * 512 + 512], x_t(0, k),
                                    ALU.subtract).then_inc(s_w0l, 1)
                e.wait_ge(s_hi, 2)
                e.tensor_tensor(ring_t(0, 1)[:, 512:1024], raw[:, 0, 512:1024], ring_t(0, 0)[:, 512:1024],
                                ALU.subtract).then_inc(s_lo, 2)
                return
            e.wait_ge(s_hi, i + 1)
            e.tensor_tensor(piece_dst(i, 1), raw_t(i), piece_dst(i, 0), ALU.subtract).then_inc(s_lo, 1)

        for i, (kind, a, b) in enumerate(pieces):
            if kind == "w":
                key = a * NU + b - RW if (a, b) != (0, 0) else -7
            elif kind == "x":
                key = -6 + i * 0.01 if a == 0 else (a - 1) * NU + XAT[b] - RW - 0.1
            elif (a, b) in EARLY:
                key = (NG - 1) * NU + EARLY[a, b] - RW - 0.1
            else:
                break
            act.add(key + 0.5, split_hi, i)
            dve.add(key + 0.55, split_lo, i)

        def grp(ap, off):
            return ap[:, 0:38 * 32].rearrange("p (q m) -> p q m", m=32)[:, :, off:off + 16]

        def a_hi(e, g):
            e.wait_ge(s_ar, 32 * (g + 1))
            e.wait_ge(s_init, 1)
            e.wait_ge(s_ba, 1)
            if g:
                e.wait_ge(s_pe, unit_down(g - 1, 0, 1) + 1)
            for b in range(2):
                e.activation(grp(a_t(b), 0), araw[:, b, :].rearrange("p (q m) -> p q m", m=16),
                             ACT.Copy).then_inc(s_lh, 1)

        def a_lo(e, g):
            for b in range(2):
                e.wait_ge(s_lh, 2 * g + b + 1)
                e.tensor_tensor(grp(a_t(b), 16), araw[:, b, :].rearrange("p (q m) -> p q m", m=16),
                                grp(a_t(b), 0), ALU.subtract).then_inc(s_ll, 1)

        def b_hi(e, n):
            e.wait_ge(s_braw[n % 2], braw_value(n))
            if n >= 2:
                e.wait_ge(s_pe, b_use((n - 2) // 26, (n - 2) % 26) + 1)
            e.activation(b_t(n % 2), braw[:, n % 2, :], ACT.Copy).then_inc(s_bh, 1)

        def b_lo(e, n):
            e.wait_ge(s_bh, n + 1)
            m = b_t(n % 2)[32:64, :]
            e.tensor_tensor(m, braw[32:64, n % 2, :], m, ALU.subtract).then_inc(s_bl, 1)

        def t_hi(e, g):
            e.wait_ge(s_t, 2 * g + 1)
            for q in range(2):
                for r in range(2):
                    e.activation(TT[32 * r:32 * r + 32, q, :], PS[32 * q:32 * q + 32, 2, :], ACT.Copy,
                                 scale=0.5).then_inc(s_th, 1)

        def t_lo(e, g):
            e.wait_ge(s_th, 6 * g + 4)
            for q in range(2):
                e.scalar_tensor_tensor(out=TT[64:96, q, :], in0=PS[32 * q:32 * q + 32, 2, :], scalar=0.5,
                                       in1=TT[0:32, q, :], op0=ALU.mult, op1=ALU.subtract).then_inc(s_tl, 1)

        def td_hi(e, g):
            e.wait_ge(s_t, 2 * g + 2)
            for r in range(2):
                e.activation(TT[32 * r:32 * r + 32, 2, :], PS[0:32, 4, :], ACT.Copy, scale=0.5).then_inc(s_th, 1)

        def td_lo(e, g):
            e.wait_ge(s_th, 6 * g + 6)
            e.scalar_tensor_tensor(out=TT[64:96, 2, :], in0=PS[0:32, 4, :], scalar=0.5, in1=TT[0:32, 2, :],
                                   op0=ALU.mult, op1=ALU.subtract).then_inc(s_tl, 1)

        def silu(e, g, c):
            n = g * NC + c
            e.wait_ge(s_pe, unit_gate(g, c) + 1)
            if n >= 2:
                e.wait_ge(s_a, n - 1)
            bank = 2 * (c % 2)
            if c < NC - 1:
                e.activation(sbuf2[:, c % 2, :], PS[:, bank, :], ACT.Silu).then_inc(s_silu, 1)
            else:
                e.wait_ge(s_act, n)
                e.activation(sbuf2[0:64, c % 2, :], PS[0:64, bank, :], ACT.Silu).then_inc(s_silu, 1)
                e.activation(sbuf2[0:64, 2, :], PS[64:128, bank, :], ACT.Copy).then_inc(s_u21, 1)

        def gated(e, g, c):
            n = g * NC + c
            e.wait_ge(s_silu, n + 1)
            if n >= 2:
                e.wait_ge(s_act, n - 1)
            if c < NC - 1:
                e.wait_ge(s_pe, unit_up(g, c) + 1)
                e.tensor_tensor(sbuf2[:, 2 + c % 2, :], sbuf2[:, c % 2, :], PS[:, 2 * (c % 2) + 1, :],
                                ALU.mult).then_inc(s_a, 1)
            else:
                e.wait_ge(s_u21, g + 1)
                e.tensor_tensor(sbuf2[0:64, 2 + c % 2, :], sbuf2[0:64, c % 2, :], sbuf2[0:64, 2, :],
                                ALU.mult).then_inc(s_a, 1)

        def act_hi(e, g, c):
            n = g * NC + c
            e.wait_ge(s_a, n + 1)
            p = 128 if c < NC - 1 else 64
            e.activation(act_t(c, 0)[0:p, :], sbuf2[0:p, 2 + c % 2, :], ACT.Copy).then_inc(s_ah, 1)

        def act_lo(e, g, c):
            n = g * NC + c
            e.wait_ge(s_ah, n + 1)
            if c < NC - 1:
                dst, p = act_t(c, 1), 128
            else:
                dst, p = act_t(c, 0)[64:128, :], 64
            e.tensor_tensor(dst, sbuf2[0:p, 2 + c % 2, :], act_t(c, 0)[0:p, :], ALU.subtract).then_inc(s_act, 1)

        def y_out(e, g, h, tt, s):
            if tt < 3:
                e.wait_ge(s_z, g * 6 + h * 3 + tt + 1)
            else:
                e.wait_ge(s_pe, unit_down(g, h, 10) + 1)
            if g and h == 0:
                e.wait_ge(s_yst, 32 * g)
                e.wait_ge(s_lm, 64 * g)
            dst = ybuf[:, tt, h * 512:(h + 1) * 512]
            if s is s_ya:
                e.activation(dst, PS[:, 4 * h + tt, :], ACT.Copy).then_inc(s, 1)
            else:
                e.tensor_copy(dst, PS[:, 4 * h + tt, :]).then_inc(s, 1)

        def lt_copy(e, m):
            q, h, slot = LT[m]
            e.wait_ge(s_lt, m + 1)
            e.wait_ge(s_lm, 64 * NG - 32)
            if m >= 2:
                e.wait_ge(s_lg, m - 1)
            e.activation(ytp[:, slot * 512:(slot + 1) * 512], PS[:, slot, :], ACT.Copy).then_inc(s_lc, 1)

        def best(e, q, t, n):
            e.wait_ge(s_L, n)
            for r in range(q, q + t):
                m = e.max(mx[:, r, :], Lg[:, r, :])
            m.then_inc(s_L, 1)
            e.wait_ge(s_L, n + 1)
            for r in range(q, q + t):
                m = e.max_index(mi[:, r, :], mx[:, r, :], Lg[:, r, :])
            m.then_inc(s_L, 1)

        def choice(e, g):
            e.wait_ge(s_L, 4 * (g + 1) if g < NG - 1 else 18)
            ts = slice(4 * g, 4 * g + 4)
            ids = mi[:, ts, 0:2].rearrange("p t (s o) -> p s t o", o=1)
            e.tensor_tensor(oh[:, :, ts, :], io8.rearrange("p (a b e) -> p a b e", a=1, b=1).to_broadcast([128, 2, 4, 8]),
                            ids.to_broadcast([128, 2, 4, 8]), ALU.is_equal).then_inc(s_oe, 1)
            e.wait_ge(s_oe, g + 1)
            e.tensor_tensor(msk[:, ts, :], oh[:, 0, ts, :], oh[:, 1, ts, :], ALU.add).then_inc(s_m, 1)

        def l_step(e, g, o):
            s, tt = divmod(o, 4)
            h, x = divmod(s, 8)
            n = 64 * g + o
            if o == 0:
                e.wait_ge(s_ya, 4 * (g + 1) - (2 if g == NG - 1 else 0))
                e.wait_ge(s_yd, 4 * (g + 1) - (2 if g == NG - 1 else 0))
            if tt == 0:
                e.wait_ge(s_wb[s % 2], 16 * (8 * g + s // 2 + 1))
            if n >= 3:
                e.wait_ge(s_lm, n - 2)
            e.tensor_tensor_reduce(out=PS[:, (5 if g < NG - 1 else 1) + n % 3, :], in0=ybuf[:, tt, h * 512:(h + 1) * 512],
                                   in1=ytp[:, (s % 2) * 512:(s % 2) * 512 + 512], scale=1.0, scalar=0.0,
                                   op0=ALU.mult, op1=ALU.add, accum_out=Lp[:, h, tt, x:x + 1]).then_inc(s_lm, 1)

        def l_sum(e, g):
            e.wait_ge(s_lm, 64 * (g + 1))
            if g == 0:
                e.wait_ge(s_cb, 80)
            lg = Lg[:, 4 * g:4 * g + 4, :]
            e.tensor_tensor(lg, Lp[:, 0], Lp[:, 1], ALU.add).then_inc(s_L, 1)
            e.wait_ge(s_L, 4 * g + 1)
            e.tensor_tensor(lg, lg, bg_s[:, :].rearrange("p (o b) -> p o b", o=1).to_broadcast([128, 4, 8]),
                            ALU.add).then_inc(s_L, 1)
            best(e, 4 * g, 4, 4 * g + 2)

        def l_add(e, q):
            if q > 12:
                e.wait_ge(s_lg, LT_AT[q + 1, 1] + 1)
            n = 12 + 3 * ((q - 12) // 2)
            if q == 12:
                e.wait_ge(s_lm, 64 * NG - 32)
                e.tensor_tensor(Lp[:, 1], Lp[:, 0], bg_s[:, :].rearrange("p (o b) -> p o b", o=1)
                                .to_broadcast([128, 4, 8]), ALU.add).then_inc(s_lb, 1)
                e.wait_ge(s_lg, LT_AT[q + 1, 1] + 1)
                e.wait_ge(s_lb, 1)
            col = 8 * (q % 4)
            e.tensor_tensor(Lg[:, q:q + 2, :],
                            PS[:, 2 + (q - 12) // 2, col:col + 16].rearrange("p (a b) -> p a b", b=8),
                            Lp[:, 1, q - 12:q - 10, :], ALU.add).then_inc(s_L, 1)
            best(e, q, 2, n + 1)

        for g in range(NG):
            a_key = -4.0 if g == 0 else unit_down(g - 1, 0, 3)
            act.add(a_key, a_hi, g)
            dve.add(a_key, a_lo, g)
            act.add(g * NU - 0.25, t_hi, g)
            dve.add(g * NU - 0.24, t_lo, g)
            act.add(unit_down(g, 0, 0) + 0.6, td_hi, g)
            dve.add(unit_down(g, 0, 0) + 0.61, td_lo, g)
            for i in range(26):
                n = g * 26 + i
                key = -0.45 + 0.01 * n if n < 2 else b_use((n - 2) // 26, (n - 2) % 26) + 0.7
                act.add(key, b_hi, n)
                dve.add(key + 0.01, b_lo, n)
            for c in range(NC):
                act.add(unit_gate(g, c) + 0.1, silu, g, c)
                dve.add(unit_up(g, c) + 0.2, gated, g, c)
                act.add(unit_up(g, c) + 0.3, act_hi, g, c)
                dve.add(unit_up(g, c) + 0.4, act_lo, g, c)
            for h in range(2):
                for tt in range(4):
                    (dve if tt % 2 else act).add(unit_down(g, h, 10) + 0.2, y_out, g, h, tt, s_yd if tt % 2 else s_ya)
            if g < NG - 1:
                for o in range(64):
                    dve.add((g + 1) * NU + logit_unit(o) + 0.6, l_step, g, o)
                dve.add((g + 1) * NU + logit_unit(63) + 0.65, l_sum, g)
                dve.add((g + 1) * NU + logit_unit(63) + 0.66, choice, g)
        for o in range(32):
            dve.add(unit_down(NG - 1, 0, 10) + o // 4 + 0.6, l_step, NG - 1, o)
        for q in range(12, 16):
            act.add(unit_down(NG - 1, 1, 10) + 0.2, lt_copy, LT_AT[q, 1])
            if q % 2:
                dve.add(unit_down(NG - 1, 1, 10) + 0.3, l_add, q - 1)
        dve.add(unit_down(NG - 1, 1, 10) + 0.31, choice, NG - 1)

        def blk_hi(e, b):
            if b == 0:
                e.wait_ge(s_f, 1)
                e.activation(ring_t(0, 0)[:, 0:512], PS[:, 6, :], ACT.Copy).then_inc(s_f0, 1)
                e.wait_ge(s_tp, 1)
                e.activation(ring_t(0, 0)[:, 512:1024], PS[:, 7, :], ACT.Copy).then_inc(s_tc, 1)
                return
            e.wait_ge(s_tp, b + 1)
            if b >= 2:
                e.wait_ge(s_blk, b)
            tp = PS[:, 2 * (b % 2):2 * (b % 2) + 2, :].rearrange("p a n -> p (a n)")
            e.wait_ge(s_tlo, b)
            e.activation(ytp[:, :], tp, ACT.Copy)
            e.activation(ring_t(b % 2, 0), tp, ACT.Copy).then_inc(s_tc, 1)

        def blk_out(e, b):
            e.wait_ge(s_blk, b + 2)
            if b >= 2:
                e.wait_ge(s_sc, 16 * (b - 1))
            z = PS[:, 4 + 2 * (b % 2):6 + 2 * (b % 2), :]
            y = sbuf2[:, 2 * (b % 2):2 * (b % 2) + 2, :]
            e.activation(y, z, ACT.Copy).then_inc(s_zc, 1)
            e.wait_ge(s_ba, b + 2)
            e.activation(y, y, ACT.Relu, scale=0.5).then_inc(s_zr, 1)

        def blocks_in_use(e):
            e.wait_ge(s_meta, 1)
            return e.value_load(meta[0:1, 3 * NB + 7:3 * NB + 8], min_val=32, max_val=NB)

        def when(e, used, b, fn, *args):
            if b < 32:
                fn(*args)
            elif b < NB:
                with e.If(used > b):
                    fn(*args)

        @block.gpsimd
        def _(e):
            e.memset(R[:, LO:LO + LA].bitcast(F32), 0.0).then_inc(s_init, 1)
            e.memset(R[:, LO + LA:RN].bitcast(F32), 0.0).then_inc(s_ba, 1)
            pool.run(e)
            block_hots(e)
            y_lo(e, 1)
            gather_y(e, 2)
            add_bias(e, 0)
            gather_y(e, 3)
            scatter(e, 0)
            used = blocks_in_use(e)
            for b in range(1, NB):
                when(e, used, b + 1, y_lo, e, b + 1)
                when(e, used, b + 3, gather_y, e, b + 3)
                when(e, used, b, add_bias, e, b)
                when(e, used, b, scatter, e, b)
            e.wait_ge(s_sc, e.value_load(meta[0:1, 3 * NB + 6:3 * NB + 7], min_val=16 * 32, max_val=16 * NB))

        @block.scalar
        def _(e):
            act.run(e)
            blk_hi(e, 0)
            blk_hi(e, 1)
            blk_out(e, 0)
            used = blocks_in_use(e)
            for b in range(2, NB):
                when(e, used, b, blk_hi, e, b)
                when(e, used, b - 1, blk_out, e, b - 1)
            when(e, used, NB - 1, blk_out, e, NB - 1)

        def linker(e, n):
            n = [n]

            def link(ins):
                n[0] += 1
                ins.then_inc(s_v, 1)
                e.wait_ge(s_v, n[0])
            return link

        def adapter_rows(e):
            link = linker(e, 0)
            e.wait_ge(s_c, 32)
            link(e.tensor_copy(loraf[:, :], lorai[:, :]))
            link(e.scalar_tensor_tensor(out=idx_a[:, :], in0=loraf[:, :], scalar=128.0,
                                        in1=ci[:, 24:25].to_broadcast([128, 8]), op0=ALU.mult, op1=ALU.add))
            l3 = loraf[:, :].rearrange("p (b o) -> p b o", o=1)
            link(e.scalar_tensor_tensor(out=idx_b[:, :, :], in0=l3.to_broadcast([128, 8, NC]), scalar=352.0,
                                        in1=cB.rearrange("p (o c) -> p o c", o=1).to_broadcast([128, 8, NC]),
                                        op0=ALU.mult, op1=ALU.add))
            e.scalar_tensor_tensor(out=idx_d[:, :, :], in0=l3.to_broadcast([128, 8, 2]), scalar=32.0,
                                   in1=cD.rearrange("p (o c) -> p o c", o=1).to_broadcast([128, 8, 2]),
                                   op0=ALU.mult, op1=ALU.add).then_inc(s_idx, 3)

        dve.add(-5.435, adapter_rows)

        e_or = AB[:, 1024:1792].bitcast(BF16).rearrange("p (t r) -> p t r", r=128)
        e_ob = AB[:, 1792:1816].bitcast(BF16).rearrange("p (t a b) -> p t a b", t=ET, a=2)
        e_before = AB[:, 1820:1834]
        e_rank = AB[:, 1834:1846]
        e_pm = AB[:, 1846:1860]
        short = loraf[:, 0:1]

        def rows_of(e, link, pm_a, pm_b, pm, lo, hi, done):
            n = hi - lo
            link(e.tensor_copy(pm[:, 0:n], pm_a))
            link(e.tensor_tensor(pm[:, 0:n], pm[:, 0:n], pm_b, ALU.add))
            e.tensor_scalar(gidx[:, lo:hi], pm[:, 0:n], -1.0, 0.0, ALU.add, ALU.max).then_inc(done, 1)
            link(e.tensor_scalar(pm[:, n:2 * n], pm[:, 0:n], 0.0, dump, ALU.is_equal, ALU.mult))
            e.scalar_tensor_tensor(out=sidx[:, lo:hi], in0=pm[:, 0:n], scalar=-1.0, in1=pm[:, n:2 * n],
                                   op0=ALU.add, op1=ALU.add).then_inc(done, 1)

        def early_hots(e):
            link = linker(e, 3)
            e.wait_ge(s_ll, 2 * NG)
            e.wait_ge(s_ep, 1)
            link(e.memset(e_before, 0.0))
            for t in range(ET):
                link(e.tensor_tensor(e_before[:, t + 1:t + 2], e_before[:, t:t + 1], PS[:, 5, t:t + 1], ALU.add))
            link(e.tensor_scalar(short, e_before[:, ET:ET + 1], -1.0, 256.0, ALU.mult, ALU.add))
            link(e.tensor_scalar(short, short, 0.0, None, ALU.max))
            link(e.tensor_tensor(e_rank, e_before[:, 0:ET], PS[:, 5, 16:16 + ET], ALU.add))
            link(e.scalar_tensor_tensor(out=e_rank, in0=msk[:, 0:ET, 0], scalar=-4096.0, in1=e_rank,
                                        op0=ALU.mult, op1=ALU.add))
            with nc.allow_low_precision(reason="whole numbers under 2^13"):
                link(e.tensor_scalar(posi[:, 0, 0:ET], e_rank, 4096.0, None, ALU.add))
            e.tensor_scalar(posi[:, 1, 0:ET], posi[:, 0, 0:ET], 7, None, ALU.logical_shift_right)
            link(e.tensor_scalar(posi[:, 2, 0:ET], posi[:, 0, 0:ET], 127, None, ALU.bitwise_and))
            for a in range(2):
                link(e.tensor_tensor(e_ob[:, :, a], io_b[:, 0:2].rearrange("p (o b) -> p o b", o=1).to_broadcast([128, ET, 2]),
                                     posi[:, 1, 0:ET].rearrange("p (t o) -> p t o", o=1).to_broadcast([128, ET, 2]),
                                     ALU.is_equal))
            e.tensor_tensor(e_ob[:, :, 0], e_ob[:, :, 0],
                            thr[:, 0:ET].rearrange("p (t b) -> p t b", b=1).to_broadcast([128, ET, 2]), ALU.mult)
            link(e.tensor_tensor(e_ob[:, :, 1], e_ob[:, :, 1],
                                 tok1[:, 0:1].rearrange("p (t b) -> p t b", b=1).to_broadcast([128, ET, 2]), ALU.mult))
            e.tensor_tensor(e_or, io128.rearrange("p (o r) -> p o r", o=1).to_broadcast([128, ET, 128]),
                            posi[:, 2, 0:ET].rearrange("p (t o) -> p t o", o=1).to_broadcast([128, ET, 128]),
                            ALU.is_equal).then_inc(s_ee, 1)

        E_LINKS = 3 + 1 + ET + 5 + 1 + 2 + 1

        def early_rows(e):
            e.wait_ge(s_ep, 2)
            rows_of(e, linker(e, E_LINKS), PS[:, 5, 32:34], PS[:, 5, 34:36], e_pm, 0, 2, s_ee)

        dve.add(unit_down(NG - 1, 0, 1) + 0.62, early_hots)
        dve.add(unit_down(NG - 1, 0, 4) + 0.62, early_rows)

        @block.vector
        def _(e):
            dve.run(e)
            link = linker(e, E_LINKS + 3)

            def bc(ap, shape):
                return ap.to_broadcast(shape)

            e.wait_ge(s_f0, 1)
            e.tensor_tensor(ring_t(0, 1)[:, 0:512], PS[:, 6, :], ring_t(0, 0)[:, 0:512], ALU.subtract).then_inc(s_f1, 1)
            e.wait_ge(s_tc, 1)
            e.tensor_tensor(ring_t(0, 1)[:, 512:1024], PS[:, 7, :], ring_t(0, 0)[:, 512:1024],
                            ALU.subtract).then_inc(s_tlo, 1)

            e.wait_ge(s_rk, 1)
            e.wait_ge(s_yst, 16 * (2 * NG - 1))
            e.wait_ge(s_y0, 16)
            rk = PS[:, 0, 0:136].rearrange("p (t e) -> p t e", e=8)
            cmp1 = RT[:, 256:384].rearrange("p (e j) -> p e j", j=16)
            cmp2 = RT[:, 256:384].rearrange("p (e j) -> p e j", j=8)
            nb = RT[:, 660:668]
            cb, cbx = RT[:, 392:400], RT[:, 400:408]
            n_e = RT[:, 384:392]
            e.tensor_copy(n_e[:, 1:8], rk[:, 16, 1:8])
            link(e.tensor_tensor(n_e[:, 0:1], rk[:, 16, 0:1], short, ALU.add))
            link(e.tensor_tensor(cmp1, bc(n_e.rearrange("p (e o) -> p e o", o=1), [128, 8, 16]),
                                 bc(thr.rearrange("p (o j) -> p o j", o=1), [128, 8, 16]), ALU.is_gt))
            link(e.tensor_reduce(nb, cmp1, AX.X, ALU.add))
            link(e.tensor_tensor(cmp2, bc(nb.rearrange("p (o j) -> p o j", o=1), [128, 16, 8]),
                                 tri.rearrange("p (e j) -> p e j", j=8), ALU.mult))
            link(e.tensor_reduce(RT[:, 392:408], cmp2, AX.X, ALU.add))
            R2 = RT[:, 408:536].rearrange("p (t e) -> p t e", e=8)
            link(e.scalar_tensor_tensor(out=R2, in0=bc(cbx.rearrange("p (o e) -> p o e", o=1), [128, 16, 8]),
                                        scalar=128.0, in1=rk[:, 0:16, :], op0=ALU.mult, op1=ALU.add))
            link(e.tensor_scalar(R2[:, ET:16, 0], R2[:, ET:16, 0], short, None, ALU.add))
            at_row = RT[:, 0:256].rearrange("p (s t e) -> p s t e", s=2, e=8)
            link(e.tensor_tensor(at_row, oh[:, :, :, :], bc(R2.rearrange("p (o t) e -> p o t e", o=1), [128, 2, 16, 8]),
                                 ALU.mult))
            with nc.allow_low_precision(reason="whole numbers under 2^13"):
                link(e.tensor_reduce(posi[:, 0, :].rearrange("p (s t) -> p s t", s=2), at_row, AX.X, ALU.add))
            e.tensor_scalar(posi[:, 1, :], posi[:, 0, :], 7, None, ALU.logical_shift_right)
            link(e.tensor_scalar(posi[:, 2, :], posi[:, 0, :], 127, None, ALU.bitwise_and))
            for q in range(0, 32, 8):
                if q == 0:
                    e.wait_ge(s_y1, 48)
                if q % 16 == 0:
                    e.tensor_tensor(OB[:, q // 16, :, 0], bc(io_b.rearrange("p (o b) -> p o b", o=1), [128, 16, NB]),
                                    bc(posi[:, 1, q:q + 16].rearrange("p (t o) -> p t o", o=1), [128, 16, NB]),
                                    ALU.is_equal).then_inc(s_pos, 1)
                e.tensor_tensor(OR[:, q:q + 8, :], bc(io128.rearrange("p (o r) -> p o r", o=1), [128, 8, 128]),
                                bc(posi[:, 2, q:q + 8].rearrange("p (q o) -> p q o", o=1), [128, 8, 128]),
                                ALU.is_equal).then_inc(s_oh, 1)
            eb = RT[:, 536:577]
            cm2 = RT[:, 0:8 * NB].rearrange("p (b e) -> p b e", e=8)
            link(e.tensor_tensor(cm2, bc(io_b.rearrange("p (b o) -> p b o", o=1), [128, NB, 8]),
                                 bc(cb.rearrange("p (o e) -> p o e", o=1), [128, NB, 8]), ALU.is_ge))
            link(e.tensor_reduce(eb, cm2, AX.X, ALU.add))
            link(e.tensor_scalar(eb, eb, 7.0, None, ALU.min))
            link(e.tensor_copy(meta[:, 2 * NB:3 * NB], eb))
            link(e.tensor_scalar(meta[:, 0:NB], meta[:, 2 * NB:3 * NB], 1, None, ALU.bitwise_and))
            link(e.tensor_scalar(meta[:, 2 * NB:3 * NB], eb, 16.0, 16.0, ALU.mult, ALU.add))
            link(e.tensor_scalar(meta[:, NB:2 * NB], eb, 8.0, float(NP - 56), ALU.mult, ALU.add))
            link(e.tensor_scalar(meta[:, 3 * NB + 6:3 * NB + 7], cb[:, 7:8], 16.0, None, ALU.mult))
            link(e.tensor_copy(meta[:, 3 * NB + 7:3 * NB + 8], cb[:, 7:8]))
            e.tensor_scalar(meta[:, 3 * NB:3 * NB + 6], cb[:, 0:6], 1.0, None, ALU.add).then_inc(s_meta, 1)
            e.wait_ge(s_rk, 2)
            rows_of(e, link, PS[:, 1, 2:NB], PS[:, 1, NB + 2:2 * NB], RT[:, 577:655], 2, NB, s_pm)

            for ex in range(1, NE):
                if ex >= 2:
                    e.wait_ge(s_blk, e.value_load(meta[0:1, 3 * NB + ex - 2:3 * NB + ex - 1], min_val=1, max_val=NB + 1))
                for k in range(8):
                    if (ex, k) in EARLY:
                        continue
                    i = at[("e", ex, k)]
                    arrived(e, i)
                    link(e.tensor_copy(s_w_t(ex, k, 0), raw[:, i % RW, :]))
                    e.tensor_tensor(s_w_t(ex, k, 1), raw[:, i % RW, :], s_w_t(ex, k, 0), ALU.subtract).then_inc(s_lo, 1)


        @block.tensor
        def _(e):
            def mm3(out_, hi, lo, whi, wlo, start, stop=False):
                e.matmul(out_, hi, whi, start=start, stop=False)
                e.matmul(out_, hi, wlo, start=False, stop=False)
                return e.matmul(out_, lo, whi, start=False, stop=stop)

            def lora_in(g):
                e.wait_ge(s_ll, 2 * g + 2)
                for b in range(2):
                    for k in range(8):
                        for part in range(2):
                            m = e.matmul(PS[:, 2, b * 256:(b + 1) * 256], a_t(b)[:, k * 64:k * 64 + 128],
                                         x_t(part, k)[:, b * 256:(b + 1) * 256], start=(k == 0 and part == 0),
                                         stop=(k == 7 and part == 1))
                m.then_inc(s_t, 1)

            def lora_out(g, c, bank, q, last):
                n = g * 26 + c
                e.wait_ge(s_bl, n + 1)
                e.wait_ge(s_tl, 3 * g + 2)
                for b in range(2):
                    o = b * 256 + q * 128
                    m = e.matmul(PS[:, bank, b * 256:(b + 1) * 256], b_t(n % 2)[:, o:o + 128],
                                 TT[:, q, b * 256:(b + 1) * 256], start=False, stop=last and b == 1)
                return m

            def first(g, c, q):
                n = g * NU + 2 * c + q
                bank = 2 * (c % 2) + q
                m0 = g * NC + c
                e.wait_ge(*((s_w0l, 1) if n == 0 else (s_lo, at[("w", g, 2 * c + q)] + 1)))
                if m0 >= 2:
                    if q == 0:
                        e.wait_ge(s_silu, m0 - 1)
                    else:
                        e.wait_ge(s_a, m0 - 1)
                if c % 2 == 0 and g:
                    e.wait_ge(s_u21, g)
                if c == 0 and g:
                    e.wait_ge(s_ya, 4 * g - 2)
                    e.wait_ge(s_yd, 4 * g - 2)
                w = [ring_t(n, 0), ring_t(n, 1)]
                for k in range(8):
                    sl = slice(k * 128, (k + 1) * 128)
                    if n == 0 and k < 2:
                        e.wait_ge(s_w0l, 2 + k)
                    elif c == 0 and q == 0 and k % 2 == 0:
                        e.wait_ge(s_lo, at[("x", g, k // 2)] + 1)
                    e.matmul(PS[:, bank, :], w[0][:, sl], x_t(0, k), start=(k == 0), stop=False)
                    e.matmul(PS[:, bank, :], w[0][:, sl], x_t(1, k), start=False, stop=False)
                    e.matmul(PS[:, bank, :], w[1][:, sl], x_t(0, k), start=False, stop=False)
                if c == NC - 1:
                    lora_out(g, c, bank, 0, False)
                    lora_out(g, c, bank, 1, True).then_inc(s_pe, 1)
                elif c == 0:
                    if q == 0:
                        lora_in(g)
                    else:
                        lora_out(g, 0, 0, 0, True).then_inc(s_pe, 1)
                        lora_out(g, 0, 1, 1, True).then_inc(s_pe, 1)
                else:
                    lora_out(g, c, bank, q, True).then_inc(s_pe, 1)

            def lora_down_in(g, c):
                e.wait_ge(s_act, g * NC + c + 1)
                if c == 0 and g:
                    e.wait_ge(s_ya, 4 * g)
                for part in range(2 if c < NC - 1 else 1):
                    for b in range(2):
                        m = e.matmul(PS[:, 4, b * 256:(b + 1) * 256], a_t(b)[:, (16 + c) * 32:(16 + c) * 32 + 128],
                                     act_t(c, part)[:, b * 256:(b + 1) * 256],
                                     start=(c == 0 and part == 0 and b == 0), stop=(c == NC - 1),
                                     skip_group_check=True)
                if c == NC - 1:
                    m.then_inc(s_t, 1)

            def down(g, h, j):
                n = unit_down(g, h, j)
                e.wait_ge(s_lo, at[("w", g, n - g * NU)] + 1)
                e.wait_ge(s_act, g * NC + 2 * j + 2 if h == 0 else g * NC + NC)
                if j == 0 and h == 0:
                    e.wait_ge(s_a, g * NC + NC - 1)
                if j == 0 and h == 1:
                    e.wait_ge(s_tl, 3 * g + 3)
                    if g:
                        e.wait_ge(s_lm, 64 * g)
                    if g == NG - 1:
                        e.wait_ge(s_ee, 3)
                w = [ring_t(n, 0), ring_t(n, 1)]

                def part(tt, cc):
                    c = 2 * j + cc
                    o = PS[:, 4 * h + tt, :]
                    ts = slice(tt * 128, (tt + 1) * 128)
                    whi, wlo = (x[:, cc * 512:(cc + 1) * 512] for x in w)
                    if c < NC - 1:
                        return mm3(o, act_t(c, 0)[:, ts], act_t(c, 1)[:, ts], whi, wlo, start=(c == 0))
                    e.matmul(o, act_t(c, 0)[:, ts], whi, start=False, stop=False)
                    return e.matmul(o, act_t(c, 0)[:, ts], wlo, start=False, stop=False)

                if j < 10:
                    for cc in range(2):
                        for tt in range(4):
                            if j == 0 and h == 0 and cc == 0 and tt == 2:
                                e.wait_ge(s_u21, g + 1)
                            m = part(tt, cc)
                    m.then_inc(s_pe, 1)
                    return
                e.wait_ge(s_tl, 3 * g + 3)
                e.wait_ge(s_bl, g * 26 + NC + 2 * h + 2)
                for tt in range(4):
                    if g == NG - 1 and h == 1:
                        if tt >= 2:
                            logit_turn(LT_AT[10 + tt, 1])
                    part(tt, 0)
                    if g == NG - 1 and h == 1 and tt == 3:
                        logit_sum(LT_AT[12, 1])
                    part(tt, 1)
                    nb_ = g * 26 + NC + 2 * h + tt // 2
                    e.matmul(PS[:, 4 * h + tt, :], TT[:, 2, tt * 128:(tt + 1) * 128], b_t(nb_ % 2),
                             start=False, stop=True).then_inc(s_z if tt < 3 else s_pe, 1)

            def logit_turn(m):
                q, h, slot = LT[m]
                g, tt = NG - 1, q % 4
                if m == 0:
                    e.wait_ge(s_cb, 80)
                if m >= 2:
                    e.wait_ge(s_lc, m - 1)
                e.wait_ge(s_lm, 64 * NG - 32)
                e.wait_ge(s_yd if tt % 2 else s_ya, 4 * g + 2 * h + tt // 2 + 1)
                for k in range(4):
                    i = e.transpose(PS[:, slot, k * 128:(k + 1) * 128],
                                    ybuf[:, tt, h * 512 + k * 128:h * 512 + (k + 1) * 128], ident[:, :])
                i.then_inc(s_lt, 1)

            def logit_sum(m):
                q, h, slot = LT[m]
                e.wait_ge(s_lc, m + 1)
                col = 8 * (q % 4)
                for k in range(4):
                    i = e.matmul(PS[:, 2 + (q - 12) // 2, col:col + 8],
                                 ytp[:, slot * 512 + k * 128:slot * 512 + (k + 1) * 128], wg_s[:, 4 * h + k, :],
                                 start=(k == 0 and q % 2 == 0), stop=(k == 3),
                                 skip_group_check=True)
                i.then_inc(s_lg, 1)

            for g in range(NG):
                for c in range(NC):
                    first(g, c, 0)
                    if c < NC - 1:
                        first(g, c, 1)
                    if c:
                        lora_down_in(g, c - 1)
                for h in range(2):
                    for j in range(11):
                        down(g, h, j)
                        if h == 0 and j == 0:
                            lora_down_in(g, NC - 1)
                        if g == NG - 1 and h == 0 and j == 1:
                            e.wait_ge(s_m, NG - 1)
                            e.matmul(PS[:, 5, 0:ET], ut[:, 128:256], msk[:, 0:ET, 0], start=True, stop=True)
                            e.matmul(PS[:, 5, 16:16 + ET], ut[:, 0:128], msk[:, 0:ET, 0],
                                     start=True, stop=True).then_inc(s_ep, 1)
                        if g == NG - 1 and h == 0 and j == 4:
                            e.wait_ge(s_ee, 1)
                            for t in range(ET):
                                m = e.matmul(PS[:, 5, 32:36], e_or[:, t, :], e_ob[:, t].rearrange("p a b -> p (a b)"),
                                             start=(t == 0), stop=(t == ET - 1))
                            m.then_inc(s_ep, 1)
            last = [LT_AT[12 + t, 1] for t in range(4)]
            logit_turn(last[2])
            logit_sum(last[1])
            logit_turn(last[3])
            logit_sum(last[2])
            logit_sum(last[3])

            def turn(b):
                if b < 2:
                    e.wait_ge(s_ge[b], 16)
                    src = early_y(b)
                else:
                    e.wait_ge(s_gd[b % 3], 16 * ((b - 2) // 3 + 1))
                    e.wait_ge(s_tc, b - 1)
                    src = ybuf[:, b % 3, :]
                bank = 2 * (b % 2) if b else 6
                for k in range(8):
                    m = e.transpose(PS[:, bank + k // 4, (k % 4) * 128:(k % 4 + 1) * 128],
                                    src[:, k * 128:(k + 1) * 128], ident[:, :])
                    if b == 0 and k == 0:
                        m.then_inc(s_blk, 1)
                    if b == 0 and k == 3:
                        m.then_inc(s_f, 1)
                m.then_inc(s_tp, 1)

            def ranks():
                e.wait_ge(s_m, 4)
                rk = PS[:, 0, 0:136].rearrange("p (t e) -> p t e", e=8)
                for t in range(16):
                    n_ = 16 - t
                    e.matmul(rk[:, t + 1:17, :], ut[:, 128:256],
                             msk[:, t:t + 1, :].to_broadcast([128, n_, 8]), start=(t == 0), stop=False,
                             skip_group_check=True)
                e.matmul(rk[:, 0:16, :], ut[:, 0:128], msk[:, :, :], start=False, stop=True,
                         skip_group_check=True).then_inc(s_rk, 1)

            def table():
                for q in range(32):
                    if q % 16 == 0:
                        e.wait_ge(s_ob, q // 8 + 2)
                    if q % 8 == 0:
                        e.wait_ge(s_oh, q // 8 + 1)
                    m = e.matmul(PS[:, 1, 0:2 * NB], OR[:, q, :], OB[:, q // 16, q % 16].rearrange("p a b -> p (a b)"),
                                 start=(q == 0), stop=(q == 31))
                m.then_inc(s_rk, 1)

            def one(b):
                if b >= 2:
                    side = e.value_load(meta[0:1, b:b + 1], min_val=0, max_val=1)
                    ready = e.value_load(meta[0:1, NB + b:NB + b + 1], min_val=NP - 56, max_val=NP)
                    off = e.snap(side * 16384)
                else:
                    off, ready = 0, at["e", 0, 7] + 1
                if b == 0:
                    e.wait_ge(s_f1, 1)
                else:
                    e.wait_ge(s_tc, b + 1)
                    e.wait_ge(s_tlo, b + 1)
                e.wait_ge(s_lo, ready)
                if b >= 2:
                    e.wait_ge(s_zc, b - 1)

                def products(ks):
                    for k in ks:
                        kk = slice(k * 128, (k + 1) * 128)
                        hi, lo = ring_t(b % 2, 0)[:, kk], ring_t(b % 2, 1)[:, kk]
                        for n in range(2):
                            o = PS[:, 4 + 2 * (b % 2) + n, :]
                            w0 = k * 2048 + n * 512
                            if b < 2:
                                w = [R[:, w0 + p * 1024:w0 + p * 1024 + 512] for p in range(2)]
                            else:
                                w = [R[:, bass.ds(off + (w0 + p * 1024), 512)] for p in range(2)]
                            m = mm3(o, hi, lo, w[0], w[1], start=(k == 0), stop=(k == 7))
                    return m

                mid = 4 if b != 1 else 5
                products(range(mid))
                if b < 31:
                    turn(b + 1)
                if b == 0:
                    e.wait_ge(s_tlo, 1)
                products(range(mid, 8)).then_inc(s_blk, 1)

            turn(0)
            ranks()
            one(0)
            table()
            one(1)
            used = blocks_in_use(e)
            for b in range(2, NB):
                if b >= 31:
                    when(e, used, b + 1, turn, b + 1)
                when(e, used, b, one, b)


def tables():
    import numpy as np

    p = np.arange(128)
    cf = np.zeros((128, 352), np.float32)
    cf[:, 0:16] = 128 * np.arange(16) + p[:, None] + 1
    cf[:, 16:24] = np.arange(8)
    cf[:, 64:80] = 128 * np.arange(16)
    e = np.arange(8)
    cf[:, 80:144] = (e[None, :] <= e[:, None]).reshape(-1)
    cf[:, 144:208] = (e[None, :] < e[:, None]).reshape(-1)
    cf[:, 208:336] = np.arange(128)
    cf[:, 336] = 2049 + p
    ci = np.zeros((128, 32), np.float32)
    ci[:, 0:22] = ((p % 16) * 22)[:, None] + np.arange(22)
    ci[:, 22:24] = ((p % 16) * 2)[:, None] + np.arange(2)
    ci[:, 24] = p
    ut = np.concatenate([(p[:, None] < p[None, :]), np.ones((128, 128), bool)], 1)
    return cf, ci, np.eye(128, dtype=np.float32), ut


def kernel(**inputs):
    import ml_dtypes
    import numpy as np
    import concourse.bacc as bacc
    from concourse import mybir as mb
    from concourse.bass_utils import run_bass_kernel_spmd as run

    A = {k: np.asarray(v) for k, v in inputs.items()}
    x = A["x"].reshape(T, H)
    xp = x.reshape(4, 512, 4, 2, 128).transpose(0, 2, 4, 3, 1).reshape(16, 128, 1024)

    def first(w):
        n = w.shape[0] // 128
        return w.reshape(n, 128, 8, 128).transpose(0, 3, 2, 1).reshape(n, 128, 1024)

    wg, wu, wd = A["L0_cond_W_gate"], A["L0_cond_W_up"], A["L0_cond_W_down"]
    g21, u21 = first(wg[:2688]), first(wu[:2688])
    both = first(np.concatenate([wg[2688:], wu[2688:]], 0))
    wdt = wd.T
    wdt = np.concatenate([wdt, wdt[2688:]], 0)
    dn = wdt.reshape(11, 2, 128, 2, 512).transpose(3, 0, 2, 1, 4).reshape(22, 128, 1024)
    wp = np.concatenate([np.stack([g21, u21], 1).reshape(42, 128, 1024), both, dn], 0)

    ag, au, ad = (A["L0_cond_A_" + n][0] for n in ("gate", "up", "down"))
    agu = np.stack([ag, au], 1).reshape(16, 2, 16, 8, 128).transpose(0, 4, 3, 1, 2).reshape(16, 128, 256)
    adt = np.concatenate([ad, ad[:, :, 2688:]], 2)
    adt = adt.reshape(16, 16, 22, 128).transpose(0, 3, 2, 1).reshape(16, 128, 352)
    at_ = np.concatenate([agu, adt], 2).reshape(2048, 608)

    bgt, but, bdt = (A["L0_cond_B_" + n][0].transpose(0, 2, 1) for n in ("gate", "up", "down"))
    z = np.zeros((16, 16, 64), np.float32)
    bgt = np.concatenate([bgt, z], 2).reshape(16, 16, 22, 1, 128)
    but = np.concatenate([but[:, :, :2688], z, but[:, :, 2688:]], 2).reshape(16, 16, 22, 1, 128)
    bgu = np.concatenate([bgt, but], 3).reshape(16 * 16 * 22, 256)
    bdn = bdt.reshape(16 * 16 * 2, 512)

    wgt = A["L0_ffn_W_gate"].reshape(8, 128, 8).transpose(1, 0, 2)
    wgb = A["L0_ffn_W_gate"].reshape(2, 512, 8).transpose(0, 2, 1).reshape(16, 512)
    we = A["L0_ffn_W_e"].reshape(8, 8, 128, 1024)
    cf, ci, ident, ut = tables()
    arrays = {
        "xp": xp, "xn": x, "wp": wp, "agu": at_, "bgu": bgu, "bdn": bdn,
        "itok": A["itok_B_2_6"], "wgt": wgt, "wgb": wgb, "bg": A["L0_ffn_b_gate"], "we": we, "be": A["L0_ffn_b_e"],
        "cst_f": cf, "cst_i": ci, "ident": ident, "ut": ut.astype(ml_dtypes.bfloat16),
    }
    arrays = {k: np.ascontiguousarray(v) for k, v in arrays.items()}
    nc = bacc.Bacc("TRN2", target_bir_lowering=False, num_devices=1, dynamic_dma_scratch_size=4096)
    args = [nc.dram_tensor(f"in_{k}", v.shape, mb.dt.from_np(v.dtype), kind="ExternalInput").ap()
            for k, v in arrays.items()]
    out = nc.dram_tensor("out_0", (T + 128, H), mb.dt.float32, kind="ExternalOutput").ap()
    build(nc, *args, out)
    r = run(nc, [{f"in_{k}": v for k, v in arrays.items()}], core_ids=[0])
    return r.results[0]["out_0"][:T].reshape(8, 256, 1024)
```
